# Optimizing a Trainium2 kernel written in Bass

```python
import numpy as np
import jax
import jax.numpy as jnp

def _softmax(x, axis=-1):
    return jax.nn.softmax(x, axis=axis)

def _gelu(x):
    return jax.nn.gelu(x, approximate=True)

def _silu(x):
    return jax.nn.silu(x)

def _sigmoid(x):
    return jax.nn.sigmoid(x)

def _layernorm(x, axis=-1, eps=1e-05):
    m = jnp.mean(x, axis=axis, keepdims=True)
    v = jnp.var(x, axis=axis, keepdims=True)
    return (x - m) / jnp.sqrt(v + eps)

def _scatter_add(tgt, idx, src, axis=0):
    return tgt.at[idx].add(src)

def _segment_sum(src, seg, n):
    return jax.ops.segment_sum(src, seg, n)
kernel_name = 'mk_adj_preln_d2_adj_r2_345490'

def setup_inputs(seed: int=0):
    np.random.seed(seed)
    _w = jnp.asarray

    def _rec_inputs():
        import jax
        import jax.numpy as jnp
        _gk = jax.random.key(seed)
        x = -0.0005963 + 1.001 * jax.random.normal(jax.random.fold_in(_gk, 1), (128, 128, 384), jnp.float32)
        _a = jax.random.bernoulli(jax.random.fold_in(_gk, 2), 0.0625, (128, 128, 128))
        _a = jnp.logical_or(_a, jnp.swapaxes(_a, -1, -2))
        _a = jnp.logical_or(_a, jnp.eye(128, dtype=bool))
        adj = _a
        return (x, adj)
    x, adj = _rec_inputs()

    def _L0_gnn_setup():
        import jax, jax.numpy as jnp
        import numpy as np
        ATT_HEAD = 12
        IN_DIM = 384
        OUT_DIM = IN_DIM // ATT_HEAD
        LEAKY_ALPHA = 0.2
        B, N = (8, 256)
        key = jax.random.key(seed)
        ks = jax.random.split(key, 8)
        feat_in = jax.random.normal(ks[0], (B, N, IN_DIM), dtype=jnp.float32)
        adj = jax.random.randint(ks[1], (B, N, N), 0, 2) > 0
        lim_W = float(np.sqrt(6.0 / (IN_DIM + OUT_DIM)))
        W = jax.random.uniform(ks[2], (ATT_HEAD, IN_DIM, OUT_DIM), minval=-lim_W, maxval=lim_W, dtype=jnp.float32)
        b = jnp.zeros((OUT_DIM,), dtype=jnp.float32)
        lim_w = float(np.sqrt(6.0 / (OUT_DIM + 1)))
        w_src = jax.random.uniform(ks[3], (ATT_HEAD, OUT_DIM, 1), minval=-lim_w, maxval=lim_w, dtype=jnp.float32)
        w_dst = jax.random.uniform(ks[4], (ATT_HEAD, OUT_DIM, 1), minval=-lim_w, maxval=lim_w, dtype=jnp.float32)
        std_H = float(np.sqrt(2.0 / (IN_DIM + IN_DIM)))
        H_w = jax.random.normal(ks[5], (IN_DIM, IN_DIM), dtype=jnp.float32) * std_H
        H_b = jax.random.normal(ks[6], (IN_DIM,), dtype=jnp.float32) * 0.01
        return {'feat_in': feat_in, 'adj': adj, 'W': W, 'b': b, 'w_src': w_src, 'w_dst': w_dst, 'H_w': H_w, 'H_b': H_b}
    _L0_gnn_all = _L0_gnn_setup()
    _L0_gnn_in = {k: v for k, v in _L0_gnn_all.items() if k in ('W', 'b', 'w_src', 'w_dst', 'H_w', 'H_b')}
    del _L0_gnn_all

    def _L1_gnn_setup():
        import jax, jax.numpy as jnp
        import numpy as np
        B, S, H = (4, 1024, 384)
        NUM_HEADS = 6
        HEAD_SIZE = H // NUM_HEADS
        NEG = -9000000000000000.0

        def _heads(x):
            b, s, _ = x.shape
            return x.reshape(b, s, NUM_HEADS, HEAD_SIZE).transpose(0, 2, 1, 3)
        key = jax.random.key(seed)
        ks = jax.random.split(key, 10)
        seq_inputs = jax.random.normal(ks[0], (B, S, H), dtype=jnp.float32)
        gm = jax.random.randint(ks[1], (B, S, S), 0, 2) > 0
        graph_mask = gm | jnp.eye(S, dtype=bool)[None]
        sc = 1.0 / np.sqrt(H)
        Wq = jax.random.normal(ks[2], (H, H), dtype=jnp.float32) * sc
        bq = jnp.zeros((H,), dtype=jnp.float32)
        Wk = jax.random.normal(ks[3], (H, H), dtype=jnp.float32) * sc
        bk = jnp.zeros((H,), dtype=jnp.float32)
        Wv = jax.random.normal(ks[4], (H, H), dtype=jnp.float32) * sc
        bv = jnp.zeros((H,), dtype=jnp.float32)
        Wf = jax.random.normal(ks[5], (H, H), dtype=jnp.float32) * sc
        bf = jnp.zeros((H,), dtype=jnp.float32)
        return {'seq_inputs': seq_inputs, 'Wq': Wq, 'bq': bq, 'Wk': Wk, 'bk': bk, 'Wv': Wv, 'bv': bv, 'Wf': Wf, 'bf': bf, 'graph_mask': graph_mask}
    _L1_gnn_all = _L1_gnn_setup()
    _L1_gnn_in = {k: v for k, v in _L1_gnn_all.items() if k in ('Wq', 'bq', 'Wk', 'bk', 'Wv', 'bv', 'Wf', 'bf')}
    del _L1_gnn_all
    return {'x': x, 'adj': adj, 'L0_gnn_W': _L0_gnn_in['W'], 'L0_gnn_b': _L0_gnn_in['b'], 'L0_gnn_w_src': _L0_gnn_in['w_src'], 'L0_gnn_w_dst': _L0_gnn_in['w_dst'], 'L0_gnn_H_w': _L0_gnn_in['H_w'], 'L0_gnn_H_b': _L0_gnn_in['H_b'], 'L1_gnn_Wq': _L1_gnn_in['Wq'], 'L1_gnn_bq': _L1_gnn_in['bq'], 'L1_gnn_Wk': _L1_gnn_in['Wk'], 'L1_gnn_bk': _L1_gnn_in['bk'], 'L1_gnn_Wv': _L1_gnn_in['Wv'], 'L1_gnn_bv': _L1_gnn_in['bv'], 'L1_gnn_Wf': _L1_gnn_in['Wf'], 'L1_gnn_bf': _L1_gnn_in['bf']}

def reference(x, adj, L0_gnn_W, L0_gnn_b, L0_gnn_w_src, L0_gnn_w_dst, L0_gnn_H_w, L0_gnn_H_b, L1_gnn_Wq, L1_gnn_bq, L1_gnn_Wk, L1_gnn_bk, L1_gnn_Wv, L1_gnn_bv, L1_gnn_Wf, L1_gnn_bf):
    import jax
    import jax.numpy as jnp

    def _L0_gnn_ref(feat_in, adj, W, b, w_src, w_dst, H_w, H_b):
        import jax, jax.numpy as jnp
        import numpy as np
        ATT_HEAD = 12
        IN_DIM = 384
        OUT_DIM = IN_DIM // ATT_HEAD
        LEAKY_ALPHA = 0.2
        B, N = (8, 256)
        h = jnp.einsum('bnd,ade->bane', feat_in, W)
        th = jnp.tanh(h)
        attn_src = jnp.einsum('bane,aeo->bano', th, w_src)
        attn_dst = jnp.einsum('bane,aeo->bano', th, w_dst)
        attn = attn_src + jnp.swapaxes(attn_dst, 2, 3)
        attn = jnp.where(attn >= 0, attn, LEAKY_ALPHA * attn)
        mask = ~adj[:, None, :, :]
        attn = jnp.where(mask, jnp.float32(-999.0), attn)
        attn = jax.nn.softmax(attn, axis=-1)
        feat_out = jnp.einsum('banm,bame->bane', attn, h) + b
        feat_out = jnp.swapaxes(feat_out, 1, 2).reshape(feat_in.shape[0], feat_in.shape[1], -1)
        feat_out = jax.nn.elu(feat_out)
        gate = jax.nn.sigmoid(feat_in @ H_w.T + H_b)
        return gate * feat_out + (1.0 - gate) * feat_in

    def _L1_gnn_ref(seq_inputs, Wq, bq, Wk, bk, Wv, bv, Wf, bf, graph_mask):
        import jax, jax.numpy as jnp
        import numpy as np
        B, S, H = (4, 1024, 384)
        NUM_HEADS = 6
        HEAD_SIZE = H // NUM_HEADS
        NEG = -9000000000000000.0

        def _heads(x):
            b, s, _ = x.shape
            return x.reshape(b, s, NUM_HEADS, HEAD_SIZE).transpose(0, 2, 1, 3)
        q = _heads(seq_inputs @ Wq + bq)
        k = _heads(seq_inputs @ Wk + bk)
        v = _heads(seq_inputs @ Wv + bv)
        scores = jnp.einsum('bhqd,bhkd->bhqk', q, k) / np.sqrt(HEAD_SIZE)
        bias = jnp.where(graph_mask, 0.0, NEG)[:, None]
        probs = jax.nn.softmax(scores + bias, axis=-1)
        ctx = jnp.einsum('bhqk,bhkd->bhqd', probs, v)
        ctx = ctx.transpose(0, 2, 1, 3).reshape(seq_inputs.shape[0], seq_inputs.shape[1], H)
        return ctx @ Wf + bf
    h = jnp.maximum(_layernorm(x, axis=-1), 0.0)
    x = x + _L0_gnn_ref(h, adj, L0_gnn_W, L0_gnn_b, L0_gnn_w_src, L0_gnn_w_dst, L0_gnn_H_w, L0_gnn_H_b)
    h = jnp.maximum(_layernorm(x, axis=-1), 0.0)
    x = x + _L1_gnn_ref(h, L1_gnn_Wq, L1_gnn_bq, L1_gnn_Wk, L1_gnn_bk, L1_gnn_Wv, L1_gnn_bv, L1_gnn_Wf, L1_gnn_bf, adj)
    return x

_drawn_inputs = setup_inputs


def setup_inputs(seed=0):
    import zlib

    import numpy as np

    out = dict(_drawn_inputs(seed))
    spreads = {'L0_gnn_b': (0.0, 0.1),
     'L1_gnn_bq': (0.0, 0.8),
     'L1_gnn_bk': (0.0, 2.0),
     'L1_gnn_bv': (0.0, 0.1),
     'L1_gnn_bf': (0.0, 0.1)}
    factors = {'L0_gnn_w_src': 12.808, 'L0_gnn_H_b': 35.324}
    for name, (base, spread) in spreads.items():
        noise = np.random.default_rng([zlib.crc32(name.encode()), seed]).standard_normal(out[name].shape)
        drawn = base * np.exp(spread * noise) if base else spread * noise
        out[name] = jnp.asarray(drawn.astype(out[name].dtype))
    for name, factor in factors.items():
        out[name] = (out[name] * factor).astype(out[name].dtype)
    return out
```

```python
from contextlib import ExitStack

import concourse.bass as bass
from concourse import mybir

ALU = mybir.AluOpType
ACT = mybir.ActivationFunctionType
AX_X = mybir.AxisListType.X
F32 = mybir.dt.float32
BF16 = mybir.dt.bfloat16
U8 = mybir.dt.uint8

P = 128
UNROLL = 4
EPS = 1e-5
MASKED0 = -999.0
NEG = -9e15
SLOPE = 0.2


def program(nc, x, adj, W, b, w_src, w_dst, HwT, H_b, Wq, bq, Wk, bk, Wv, bv, Wf, bf, out):
    NB, N, D = x.shape
    _, _, A, E = W.shape
    HEADS = 6
    DH = D // HEADS
    KC = D // P
    HP = P // DH
    HPC = P // E
    AB = 512 // N
    assert N == P and KC == 3 and A == 12 and E == 32 and HP == 2 and NB % UNROLL == 0
    SCALE = float(DH) ** -0.5

    with ExitStack() as ctx:
        def sb(name, shape, dt=F32):
            return ctx.enter_context(nc.sbuf_tensor(name, shape, dt))

        def sem(name):
            return ctx.enter_context(nc.semaphore(name))

        ident = sb("ident", [P, P])
        identb = sb("identb", [P, P], BF16)
        wcat = sb("wcat", [P, KC, A, E])
        hwt = sb("hwt", [P, KC, D])
        wq = sb("wq", [P, KC, D])
        wk = sb("wk", [P, KC, D])
        wv = sb("wv", [P, KC, D])
        wf = sb("wf", [P, KC, D])
        qkb = sb("qkb", [P, 2, KC])
        bvr = sb("bvr", [P, D])
        bfr = sb("bfr", [P, D])
        b0r = sb("b0r", [P, E])
        w_cols = sb("w_cols", [P, 2, KC])
        w_sd = sb("w_sd", [P, KC, 96])
        sel_d = sb("sel_d", [96, A, P], BF16)
        one_s = sb("one_s", [96, A, P], BF16)
        sel_b = sb("sel_b", [96, P], BF16)
        hb = sb("hb", [96, D])
        hbp = sb("hbp", [96, D], BF16)
        hbm = sb("hbm", [96, D], BF16)
        mhalf = sb("mhalf", [P, 1])

        xin = sb("xin", [P, 4, D])
        adj8 = sb("adj8", [P, 4, N], U8)
        maskb = sb("maskb", [P, 4, N], BF16)
        h0 = sb("h0", [P, 4, D])
        xh = sb("xh", [P, 2, D])
        tg = sb("tg", [P, 2, D])
        sg = sb("sg", [P, 2, D])
        hq = sb("hq", [P, 2, D])
        c0 = sb("c0", [P, 2, D])
        h0T = sb("h0T", [P, 2, KC, N])
        th = sb("th", [P, 2, D])
        thT = sb("thT", [P, 2, KC, N])
        hp = sb("hp", [P, 2, A, E + 1])
        sd32 = sb("sd32", [96, 2, N])
        sdm = sb("sdm", [96, 2, N], BF16)
        sdp = sb("sdp", [96, 2, N], BF16)
        u2 = sb("u2", [P, 2, A, N])
        lk = sb("lk", [P, 2, A, N])
        p0 = sb("p0", [P, 2, A, N])
        p0T = sb("p0T", [P, 2, A, N])
        mx0 = sb("mx0", [P, 2, A])
        rd0 = sb("rd0", [P, 2, A])
        feat = sb("feat", [P, 2, D])
        fneg = sb("fneg", [P, 2, D])
        fexp = sb("fexp", [P, 2, D])
        fg = sb("fg", [P, 2, D])
        eg = sb("eg", [P, 2, D])
        x1 = sb("x1", [P, 2, D])
        x1b = sb("x1b", [P, 2, D])
        h1 = sb("h1", [P, 2, D])
        h1T = sb("h1T", [P, 2, KC, N])
        qkT = sb("qkT", [P, 2, 2, KC, N])
        vp = sb("vp", [P, 2, HEADS, DH + 1])
        sc = sb("sc", [P, 2, HP, KC, N])
        p1 = sb("p1", [P, 2, HP, KC, N])
        p1T = sb("p1T", [P, 2, HP, KC, N])
        mx1 = sb("mx1", [P, 2, HP, KC])
        rd1 = sb("rd1", [P, 2, HEADS])
        cx = sb("cx", [P, 2, D])
        cxT = sb("cxT", [P, 2, KC, N])
        res = sb("res", [P, 2, D])
        bst = [sb(f"bst{i}", [P, 2, 6]) for i in range(2)]
        mv = [sb(f"mv{i}", [P, 2, 2]) for i in range(2)]
        ve = [sb(f"ve{i}", [P, 2, 1]) for i in range(2)]
        rstd = [sb(f"rstd{i}", [P, 2, 1]) for i in range(2)]
        nmr = [sb(f"nmr{i}", [P, 2, 1]) for i in range(2)]

        ps = ctx.enter_context(nc.psum_tensor("ps", [P, 8, 512], F32))

        def bank(i, n=N, k=KC):
            return ps[:, i, 0:k * n].rearrange("p (c n) -> p c n", n=n)

        B_H0T, B_GATE, B_H, B_SD, B_THT, B_CTXT, B_OUT, B_PV1, B_PV0, B_H1T, B_V = 4, 4, 6, 3, 3, 7, 0, 2, 5, 5, 7
        B_P1T, B_QK, B_P0T, B_SC = 0, 1, 4, 0
        Z_BANKS = (2, 3, 7)

        w_loaded = [sem(f"w_loaded{i}") for i in range(16)]
        setup_pool = sem("setup_pool")
        setup_dve = sem("setup_dve")
        x_loaded = [sem(f"x_loaded{i}") for i in range(4)]
        adj_loaded = [sem(f"adj_loaded{i}") for i in range(4)]
        stored = [sem(f"stored{i}") for i in range(2)]
        names = """bn0_done aggr0_done ve0_done rstd0_done nmr0_done h0_done xh_done mask_done
            h0T_mm h0T_done H_mm th_done hp_done gate_mm tg_done thT_mm thT_done sd_mm sdhi_done sdr1_done
            sdmid_done sdmid2_done sd_done z_mm u2a_done u2_done lka_done lk_done mx0_done sub0_done p0_done
            p0T_mm p0T_done pv0_mm rd0_done feat_done fneg_done fexp_done fg_done fc_done eg_done x1_done sg_done hq_done hg_done c0_done
            bn1_done aggr1_done ve1_done rstd1_done nmr1_done h1_done x1b_done h1T_mm h1T_done qk_mm qk_done
            v_mm v_done sc_mm mx1_done sc_done p1_done p1T_mm p1T_done pv1_mm rd1_done cx_done cxT_mm cxT_done
            out_mm res_done""".split()
        s = {n: sem(n) for n in names}

        def after(eng, name, g):
            if not isinstance(g, int) or 0 <= g < NB:
                eng.wait_ge(s[name], g + 1)

        def steps(eng, body):
            def fixed(t):
                body(t, t % UNROLL, t // UNROLL, lambda k: 0 <= t - k < NB)
            for t in range(-1, 2 * UNROLL):
                fixed(t)
            with eng.Fori(2, NB // UNROLL - 1) as turn:
                for j in range(UNROLL):
                    body(turn * UNROLL + j, j, turn, lambda k: True)
            for t in range(NB - UNROLL, NB + 3):
                fixed(t)

        block = ctx.enter_context(nc.Block())

        @block.sync
        def _(sp):
            sp.dma_start(wcat[:], W).then_inc(w_loaded[0], 16)
            sp.dma_start(w_cols[:, 0, :], w_dst).then_inc(w_loaded[1], 16)
            sp.dma_start(w_cols[:, 1, :], w_src).then_inc(w_loaded[2], 16)

            def load(g, slot):
                sp.dma_start(xin[:, slot, :], x[g]).then_inc(x_loaded[slot], 16)
                sp.dma_start(adj8[:, slot, :], adj[g]).then_inc(adj_loaded[slot], 16)
            load(0, 0)
            for n, (dst, src) in enumerate([
                    (hwt[:], HwT), (hb[:], H_b.rearrange("(o n) -> o n", o=1).to_broadcast([96, D])),
                    (b0r[:], b.rearrange("(o n) -> o n", o=1).to_broadcast([P, E])),
                    (wq[:], Wq), (wk[:], Wk), (wv[:], Wv), (wf[:], Wf),
                    (qkb[:, 0, :], bq), (qkb[:, 1, :], bk),
                    (bvr[:], bv.rearrange("(o n) -> o n", o=1).to_broadcast([P, D])),
                    (bfr[:], bf.rearrange("(o n) -> o n", o=1).to_broadcast([P, D]))]):
                sp.dma_start(dst, src).then_inc(w_loaded[3 + n], 16)
            load(1, 1)

            def body(t, j, turn, live):
                if live(-2):
                    after(sp, "xh_done", t - 2)
                    after(sp, "mask_done", t - 2)
                    load(t + 2, (j + 2) % 4)
                if live(3):
                    after(sp, "res_done", t - 3)
                    sp.dma_start(out[t - 3], res[:, (j - 3) % 2, :]).then_inc(stored[(j - 3) % 2], 16)
            steps(sp, lambda t, j, turn, live: None if isinstance(t, int) and t < 0 else body(t, j, turn, live))
            for i in range(2):
                sp.wait_ge(stored[i], 16 * (NB // 2))

        @block.gpsimd
        def _(pool):
            for n, m in enumerate((ident, identb, sel_d, one_s, sel_b)):
                nc.gpsimd.memset(m[:], 0.0).then_inc(setup_pool, 1)
            nc.gpsimd.memset(mhalf[:], -0.5).then_inc(setup_pool, 1)
            nc.gpsimd.memset(hp[:], 1.0).then_inc(setup_pool, 1)
            nc.gpsimd.memset(vp[:], 1.0).then_inc(setup_pool, 1)
            pool.wait_ge(setup_pool, 8)
            count = 8
            for m in (ident, identb):
                nc.gpsimd.affine_select(out=m[:], in_=m[:], compare_op=ALU.not_equal, fill=1.0, base=0,
                                        pattern=[[-1, P]], channel_multiplier=1).then_inc(setup_pool, 1)
                count += 1
            for r in range(3):
                for m, first in ((sel_d, 0), (one_s, A)):
                    nc.gpsimd.affine_select(out=m[:], in_=m[:], compare_op=ALU.not_equal, fill=1.0,
                                            base=-(32 * r + first), pattern=[[-1, A], [0, P]],
                                            channel_multiplier=1).then_inc(setup_pool, 1)
                    count += 1
                    pool.wait_ge(setup_pool, count)
                nc.gpsimd.affine_select(out=sel_b[:], in_=sel_b[:], compare_op=ALU.not_equal, fill=1.0,
                                        base=-32 * r, pattern=[[0, P]], channel_multiplier=1).then_inc(setup_pool, 1)
                count += 1
                pool.wait_ge(setup_pool, count)
            pool.wait_ge(w_loaded[13], 16)

            def body(t, j, turn, live):
                if live(1):
                    after(pool, "tg_done", t - 1)
                if live(0):
                    after(pool, "h0_done", t)
                    nc.gpsimd.tensor_tensor(xh[:, j % 2, :], xin[:, j, :], h0[:, j, :], ALU.add).then_inc(s["xh_done"], 1)
                if live(1):
                    g, i, k = t - 1, (j - 1) % 2, (j - 1) % 4
                    nc.gpsimd.tensor_scalar(sg[:, i, :], tg[:, i, :], 1.0, 0.5, ALU.add, ALU.mult).then_inc(s["sg_done"], 1)
                    nc.gpsimd.tensor_scalar(hq[:, i, :], h0[:, k, :], 1.0, 1.0, ALU.add, ALU.mult).then_inc(s["hq_done"], 1)
                    after(pool, "sg_done", g)
                    after(pool, "hq_done", g)
                    nc.gpsimd.tensor_tensor(hq[:, i, :], hq[:, i, :], sg[:, i, :], ALU.mult).then_inc(s["hg_done"], 1)
                    after(pool, "hg_done", g)
                    nc.gpsimd.tensor_tensor(c0[:, i, :], xh[:, i, :], hq[:, i, :], ALU.subtract).then_inc(s["c0_done"], 1)
                if live(2):
                    g, i = t - 2, (j - 2) % 2
                    after(pool, "x1_done", g)
                    after(pool, "res_done", g - 2)
                    nc.gpsimd.tensor_tensor(x1b[:, i, :], x1[:, i, :], bfr[:], ALU.add).then_inc(s["x1b_done"], 1)
                    after(pool, "ve1_done", g)
                    nc.gpsimd.tensor_tensor(rstd[1][:, i, :], ve[1][:, i, :], mhalf[:], ALU.pow).then_inc(s["rstd1_done"], 1)
                if live(-1):
                    g, i, k = t + 1, (j + 1) % 2, (j + 1) % 4
                    pool.wait_ge(adj_loaded[k], 16 * (turn + (1 if j == 3 else 0)) + 16)
                    after(pool, "sc_mm", g - 4)
                    after(pool, "ve0_done", g)
                    nc.gpsimd.tensor_tensor(rstd[0][:, i, :], ve[0][:, i, :], mhalf[:], ALU.pow).then_inc(s["rstd0_done"], 1)
                    nc.gpsimd.tensor_scalar(maskb[:, k, :], adj8[:, k, :], -1.0, -NEG, ALU.add,
                                            ALU.mult).then_inc(s["mask_done"], 1)
                if live(1):
                    g, i = t - 1, (j - 1) % 2
                    after(pool, "mx0_done", g)
                    nc.gpsimd.tensor_tensor(lk[:, i, :, :], lk[:, i, :, :],
                                            mx0[:, i, :].unsqueeze(2).to_broadcast([P, A, N]),
                                            ALU.subtract).then_inc(s["sub0_done"], 1)
            steps(pool, body)

        @block.scalar
        def _(act):
            def body(t, j, turn, live):
                a, b_, c, d = t, t - 1, t - 2, t - 3
                i0, i1 = j % 2, (j + 1) % 2
                if live(0):
                    after(act, "h0T_mm", a)
                    nc.scalar.copy(h0T[:, i0, :, :], bank(B_H0T)).then_inc(s["h0T_done"], 1)
                if live(3):
                    after(act, "p1T_mm", d)
                    nc.scalar.copy(p1T[:, i1, :, :, :],
                                   ps[:, B_P1T:B_P1T + 2, 0:KC * N].rearrange("p b (c n) -> p b c n", n=N)
                                   ).then_inc(s["p1T_done"], 1)
                if live(2):
                    after(act, "fneg_done", c)
                    nc.scalar.activation(fexp[:, i0, :], fneg[:, i0, :], ACT.Exp).then_inc(s["fexp_done"], 1)
                if live(0):
                    after(act, "H_mm", a)
                    after(act, "thT_mm", a - 2)
                    nc.scalar.activation(th[:, i0, :], ps[:, B_H, 0:D], ACT.Tanh).then_inc(s["th_done"], 1)
                    after(act, "gate_mm", a)
                    after(act, "sg_done", a - 2)
                    nc.scalar.activation(tg[:, i0, :], ps[:, B_GATE, 0:D], ACT.Tanh, scale=0.5).then_inc(s["tg_done"], 1)
                if live(3):
                    after(act, "cxT_mm", d)
                    nc.scalar.copy(cxT[:, i1, :, :], bank(B_CTXT)).then_inc(s["cxT_done"], 1)
                if live(0):
                    after(act, "thT_mm", a)
                    nc.scalar.copy(thT[:, i0, :, :], bank(B_THT)).then_inc(s["thT_done"], 1)
                if live(2):
                    after(act, "nmr1_done", c)
                    after(act, "h1T_mm", c - 2)
                    nc.scalar.activation(h1[:, i0, :], x1[:, i0, :], ACT.Relu, bias=nmr[1][:, i0, :],
                                         scale=rstd[1][:, i0, :]).then_inc(s["h1_done"], 1)
                    after(act, "h1T_mm", c)
                    nc.scalar.copy(h1T[:, i0, :, :], bank(B_H1T)).then_inc(s["h1T_done"], 1)
                if live(-1):
                    after(act, "nmr0_done", t + 1)
                    after(act, "hq_done", t - 3)
                    after(act, "xh_done", t - 3)
                    nc.scalar.activation(h0[:, (j + 1) % 4, :], xin[:, (j + 1) % 4, :], ACT.Relu,
                                         bias=nmr[0][:, i1, :], scale=rstd[0][:, i1, :]).then_inc(s["h0_done"], 1)
                if live(1):
                    after(act, "sub0_done", b_)
                    after(act, "p0T_mm", b_ - 2)
                    nc.scalar.activation(p0[:, i1, :, :], lk[:, i1, :, :], ACT.Exp).then_inc(s["p0_done"], 1)
                    after(act, "p0T_mm", b_)
                    nc.scalar.copy(p0T[:, i1, :, :],
                                   ps[:, B_P0T:B_P0T + 3, :].rearrange("p b (c n) -> p (b c) n", n=N)
                                   ).then_inc(s["p0T_done"], 1)
                if live(2):
                    after(act, "sc_done", c)
                    after(act, "p1T_mm", c - 2)
                    nc.scalar.activation(p1[:, i0, :, :, :], sc[:, i0, :, :, :], ACT.Exp, scale=SCALE).then_inc(s["p1_done"], 1)
                if live(0):
                    after(act, "z_mm", a)
                    after(act, "lk_done", a - 2)
                    nc.scalar.mul(u2[:, i0, 0:2 * AB, :],
                                  ps[:, Z_BANKS[0]:Z_BANKS[0] + 2, :].rearrange("p b (c n) -> p (b c) n", n=N),
                                  SLOPE).then_inc(s["u2a_done"], 1)
                    nc.scalar.mul(u2[:, i0, 2 * AB:A, :], bank(Z_BANKS[2], k=AB), SLOPE).then_inc(s["u2_done"], 1)
            steps(act, body)

        @block.vector
        def _(dve):
            dve.wait_ge(w_loaded[1], 16)
            dve.wait_ge(w_loaded[2], 16)
            nc.vector.memset(w_sd[:], 0.0).then_inc(setup_dve, 1)
            dve.wait_ge(setup_dve, 1)
            for c in range(KC):
                for i in range(HPC):
                    q = slice(E * i, E * i + E)
                    for k in range(2):
                        col = k * A + HPC * c + i
                        last = nc.vector.tensor_copy(
                            w_sd[q, c, :].rearrange("p (r m) -> p r m", m=32)[:, :, col:col + 1],
                            w_cols[q, k, c:c + 1].unsqueeze(2).to_broadcast([E, 3, 1]))
            last.then_inc(setup_dve, 1)

            def thirds(src, rest, mid, parts, waits):
                nc.vector.tensor_copy(parts, src).then_inc(waits[0][0], 1)
                dve.wait_ge(*waits[0])
                nc.vector.tensor_tensor(rest, src, parts, ALU.subtract).then_inc(waits[1][0], 1)
                dve.wait_ge(*waits[1])
                nc.vector.tensor_copy(mid[64:96], rest[64:96]).then_inc(waits[2][0], 1)
                nc.vector.tensor_copy(parts[32:64], rest[32:64]).then_inc(waits[3][0], 1)
                dve.wait_ge(*waits[3])
                nc.vector.tensor_tensor(parts[64:96], rest[64:96], mid[64:96],
                                        ALU.subtract).then_inc(waits[4][0], 1)

            dve.wait_ge(w_loaded[4], 16)
            thirds(hb[:], hb[:], hbm[:], hbp[:], [(setup_dve, n) for n in (3, 4, 5, 6, 7)])
            dve.wait_ge(setup_pool, 8)
            for n in (5, 10, 11, 12):
                dve.wait_ge(w_loaded[n], 16)

            def norm(k, src, g, i, between):
                nc.vector.bn_stats(bst[k][:, i, :], src).then_inc(s[f"bn{k}_done"], 1)
                after(dve, f"bn{k}_done", g)
                between()
                nc.vector.bn_aggr(mv[k][:, i, :], bst[k][:, i, :]).then_inc(s[f"aggr{k}_done"], 1)
                after(dve, f"aggr{k}_done", g)
                nc.vector.tensor_scalar(ve[k][:, i, :], mv[k][:, i, 1:2], EPS, None, ALU.add).then_inc(s[f"ve{k}_done"], 1)

            def norm_bias(k, g, i):
                after(dve, f"rstd{k}_done", g)
                nc.vector.scalar_tensor_tensor(nmr[k][:, i, :], mv[k][:, i, 0:1], -1.0, rstd[k][:, i, :],
                                               ALU.mult, ALU.mult).then_inc(s[f"nmr{k}_done"], 1)

            def body(t, j, turn, live):
                a, b_, c, d = t, t - 1, t - 2, t - 3
                i0, i1 = j % 2, (j + 1) % 2
                if live(1):
                    after(dve, "u2a_done", b_)
                    after(dve, "p0_done", b_ - 2)
                    nc.vector.scalar_tensor_tensor(
                        lk[:, i1, 0:2 * AB, :],
                        ps[:, Z_BANKS[0]:Z_BANKS[0] + 2, :].rearrange("p b (c n) -> p (b c) n", n=N), MASKED0,
                        u2[:, i1, 0:2 * AB, :], ALU.max, ALU.max).then_inc(s["lka_done"], 1)
                    after(dve, "u2_done", b_)
                    nc.vector.scalar_tensor_tensor(lk[:, i1, 2 * AB:A, :], bank(Z_BANKS[2], k=AB), MASKED0,
                                                   u2[:, i1, 2 * AB:A, :], ALU.max, ALU.max).then_inc(s["lk_done"], 1)
                if live(2):
                    pv = ps[:, B_PV0, 0:A * (E + 1)].rearrange("p (a e) -> p a e", e=E + 1)
                    after(dve, "pv0_mm", c)
                    nc.vector.reciprocal(rd0[:, i0, :], pv[:, :, E:E + 1]).then_inc(s["rd0_done"], 1)
                    after(dve, "rd0_done", c)
                    nc.vector.tensor_tensor(feat[:, i0, :].rearrange("p (a e) -> p a e", e=E), pv[:, :, 0:E],
                                            rd0[:, i0, :].unsqueeze(2).to_broadcast([P, A, E]),
                                            ALU.mult).then_inc(s["feat_done"], 1)
                    after(dve, "feat_done", c)
                    nc.vector.tensor_scalar(fneg[:, i0, :], feat[:, i0, :], 0.0, None, ALU.min).then_inc(s["fneg_done"], 1)
                if live(2):
                    after(dve, "c0_done", c)
                    nc.vector.scalar_tensor_tensor(fg[:, i0, :], feat[:, i0, :], 0.0, sg[:, i0, :], ALU.max,
                                                   ALU.mult).then_inc(s["fg_done"], 1)
                    after(dve, "fg_done", c)
                    nc.vector.tensor_tensor(fg[:, i0, :], fg[:, i0, :], c0[:, i0, :], ALU.add).then_inc(s["fc_done"], 1)
                    after(dve, "fexp_done", c)
                    nc.vector.tensor_tensor(eg[:, i0, :], fexp[:, i0, :], sg[:, i0, :], ALU.mult).then_inc(s["eg_done"], 1)
                    after(dve, "eg_done", c)
                    after(dve, "fc_done", c)
                    after(dve, "x1b_done", c - 2)
                    after(dve, "h1_done", c - 2)
                    nc.vector.tensor_tensor(x1[:, i0, :], eg[:, i0, :], fg[:, i0, :], ALU.add).then_inc(s["x1_done"], 1)

                pv1 = ps[:, B_PV1, 0:HEADS * (DH + 1)].rearrange("p (h e) -> p h e", e=DH + 1)
                if live(3):
                    after(dve, "pv1_mm", d)
                    nc.vector.reciprocal(rd1[:, i1, :], pv1[:, :, DH:DH + 1]).then_inc(s["rd1_done"], 1)

                def context():
                    if live(3):
                        after(dve, "rd1_done", d)
                        nc.vector.tensor_tensor(cx[:, i1, :].rearrange("p (h e) -> p h e", e=DH), pv1[:, :, 0:DH],
                                                rd1[:, i1, :].unsqueeze(2).to_broadcast([P, HEADS, DH]),
                                                ALU.mult).then_inc(s["cx_done"], 1)

                def values():
                    if live(0):
                        after(dve, "th_done", a)
                        nc.vector.tensor_tensor(hp[:, i0, :, 0:E], ps[:, B_H, 0:D].rearrange("p (a e) -> p a e", e=E),
                                                b0r[:].unsqueeze(1).to_broadcast([P, A, E]), ALU.add).then_inc(s["hp_done"], 1)

                if live(2):
                    after(dve, "x1_done", c)
                    norm(1, x1[:, i0, :], c, i0, context)
                else:
                    context()
                if live(-1):
                    k = (j + 1) % 4
                    dve.wait_ge(x_loaded[k], 16 * (turn + (1 if j == 3 else 0)) + 16)
                    norm(0, xin[:, k, :], t + 1, i1, values)
                else:
                    values()
                if live(2):
                    norm_bias(1, c, i0)
                if live(1):
                    after(dve, "lk_done", b_)
                    nc.vector.tensor_reduce(mx0[:, i1, :], lk[:, i1, :, :], AX_X, ALU.max).then_inc(s["mx0_done"], 1)
                if live(-1):
                    norm_bias(0, t + 1, i1)
                if live(3):
                    after(dve, "out_mm", d)
                    after(dve, "x1b_done", d)
                    if not isinstance(d, int) or d >= 2:
                        dve.wait_ge(stored[i1], 32 * turn + 16 * ((j - 3) // 2))
                    nc.vector.tensor_tensor(res[:, i1, :], ps[:, B_OUT, 0:D], x1b[:, i1, :], ALU.add).then_inc(s["res_done"], 1)
                if live(0):
                    after(dve, "sd_mm", a)
                    after(dve, "z_mm", a - 2)
                    thirds(ps[0:96, B_SD, 0:N], sd32[:, i0, :], sdm[:, i0, :], sdp[:, i0, :],
                           [(s[n], a + 1) for n in ("sdhi_done", "sdr1_done", "sdmid_done", "sdmid2_done", "sd_done")])
                if live(2):
                    after(dve, "qk_mm", c)
                    nc.vector.tensor_tensor(qkT[:, i0, :, :, :],
                                            ps[:, B_QK:B_QK + 2, 0:KC * N].rearrange("p b (c n) -> p b c n", n=N),
                                            qkb[:].unsqueeze(3).to_broadcast([P, 2, KC, N]), ALU.add).then_inc(s["qk_done"], 1)
                    after(dve, "v_mm", c)
                    nc.vector.tensor_tensor(vp[:, i0, :, 0:DH], ps[:, B_V, 0:D].rearrange("p (h e) -> p h e", e=DH),
                                            bvr[:].rearrange("p (h e) -> p h e", e=DH), ALU.add).then_inc(s["v_done"], 1)
                    scores = ps[:, B_SC:B_SC + 2, 0:KC * N].rearrange("p b (c n) -> p b c n", n=N)
                    after(dve, "sc_mm", c)
                    nc.vector.tensor_reduce(mx1[:, i0, :, :], scores, AX_X, ALU.max).then_inc(s["mx1_done"], 1)
                    after(dve, "mx1_done", c)
                    nc.vector.tensor_tensor(sc[:, i0, :, :, :], scores,
                                            mx1[:, i0, :, :].unsqueeze(3).to_broadcast([P, HP, KC, N]),
                                            ALU.subtract).then_inc(s["sc_done"], 1)
            steps(dve, body)

        @block.tensor
        def _(pe):
            mm = nc.tensor.matmul
            pe.wait_ge(setup_pool, 19)
            pe.wait_ge(setup_dve, 7)
            for n in (0, 3, 6, 7, 8, 9):
                pe.wait_ge(w_loaded[n], 16)

            def transposes(dst, src):
                for c in range(KC):
                    last = nc.tensor.transpose(dst[:, c, :], src[:, c * P:(c + 1) * P], ident[:])
                return last

            def project(dst, xT, w):
                for c in range(KC):
                    last = mm(dst, xT[:, c, :], w[:, c, :], start=(c == 0), stop=(c == KC - 1))
                return last

            def body(t, j, turn, live):
                a, b_, c, d = t, t - 1, t - 2, t - 3
                i0, i1 = j % 2, (j + 1) % 2
                if live(0):
                    after(pe, "h0_done", a)
                    transposes(bank(B_H0T), h0[:, j, :]).then_inc(s["h0T_mm"], 1)
                if live(3):
                    after(pe, "p1_done", d)
                    for h in range(HEADS):
                        last = nc.tensor.transpose(bank(B_P1T + h % 2)[:, h // 2, :], p1[:, i1, h % 2, h // 2, :], ident[:])
                    last.then_inc(s["p1T_mm"], 1)
                if live(0):
                    after(pe, "h0T_done", a)
                    project(ps[:, B_H, 0:D], h0T[:, i0], wcat[:].rearrange("p c a e -> p c (a e)")).then_inc(s["H_mm"], 1)
                if live(3):
                    after(pe, "p1T_done", d)
                    after(pe, "lka_done", t - 1)
                    for h in range(HEADS):
                        last = mm(ps[:, B_PV1, h * (DH + 1):(h + 1) * (DH + 1)], p1T[:, i1, h % 2, h // 2, :],
                                  vp[:, i1, h, :], start=True, stop=True)
                    last.then_inc(s["pv1_mm"], 1)
                if live(0):
                    mm(ps[:, B_GATE, 0:D], sel_b[:], hbp[:], start=True, stop=False)
                    for k in range(KC):
                        last = mm(ps[:, B_GATE, 0:D], h0T[:, i0, k, :], hwt[:, k, :], start=False, stop=(k == KC - 1))
                    last.then_inc(s["gate_mm"], 1)
                if live(3):
                    after(pe, "cx_done", d)
                    after(pe, "lk_done", t - 1)
                    transposes(bank(B_CTXT), cx[:, i1, :]).then_inc(s["cxT_mm"], 1)
                if live(0):
                    after(pe, "th_done", a)
                    after(pe, "lka_done", t - 1)
                    transposes(bank(B_THT), th[:, i0, :]).then_inc(s["thT_mm"], 1)
                if live(3):
                    after(pe, "cxT_done", d)
                    project(ps[:, B_OUT, 0:D], cxT[:, i1], wf).then_inc(s["out_mm"], 1)
                if live(2):
                    after(pe, "h1_done", c)
                    transposes(bank(B_H1T), h1[:, i0, :]).then_inc(s["h1T_mm"], 1)
                if live(0):
                    after(pe, "thT_done", a)
                    for k in range(KC):
                        last = mm(ps[0:96, B_SD, 0:N], w_sd[:, k, :], thT[:, i0, k, :], start=(k == 0), stop=(k == KC - 1))
                    last.then_inc(s["sd_mm"], 1)
                if live(2):
                    after(pe, "h1T_done", c)
                    for n, w in enumerate((wq, wk)):
                        for m in range(KC):
                            for k in range(KC):
                                last = mm(ps[:, B_QK + n, m * N:(m + 1) * N], w[:, k, m * P:(m + 1) * P], h1T[:, i0, k, :],
                                          start=(k == 0), stop=(k == KC - 1))
                    last.then_inc(s["qk_mm"], 1)
                    project(ps[:, B_V, 0:D], h1T[:, i0], wv).then_inc(s["v_mm"], 1)
                if live(1):
                    after(pe, "p0_done", b_)
                    after(pe, "tg_done", a)
                    after(pe, "hp_done", a)
                    for h in range(A):
                        last = nc.tensor.transpose(bank(B_P0T + h // AB, k=AB)[:, h % AB, :], p0[:, i1, h, :], ident[:])
                    last.then_inc(s["p0T_mm"], 1)
                if live(2):
                    after(pe, "res_done", t - 3)
                    after(pe, "qk_done", c)
                    mk = maskb[:, (j - 2) % 4, :].unsqueeze(1).to_broadcast([P, KC, N])
                    for n in range(HP):
                        mm(bank(B_SC + n), identb[:], mk, start=True, stop=False)
                    for h in range(HEADS):
                        q = slice(DH * (h % 2), DH * (h % 2) + DH)
                        last = mm(bank(B_SC + h % 2)[:, h // 2, :], qkT[q, i0, 0, h // 2, :], qkT[q, i0, 1, h // 2, :],
                                  start=False, stop=(h >= HEADS - HP))
                    last.then_inc(s["sc_mm"], 1)
                if live(0):
                    after(pe, "sd_done", a)
                    after(pe, "mask_done", a)
                    after(pe, "v_done", t - 2)
                    mk = maskb[:, j, :].unsqueeze(1).to_broadcast([P, AB, N])
                    for n, z in enumerate(Z_BANKS):
                        zb = bank(z, k=AB)
                        mm(zb, sdp[:, i0, :], one_s[:, n * AB:(n + 1) * AB, :], start=True, stop=False)
                        mm(zb, identb[:], mk, start=False, stop=False)
                        for h in range(AB):
                            last = mm(zb[:, h, :], sel_d[:, n * AB + h, :], sdp[:, i0, :], start=False, stop=(h == AB - 1))
                    last.then_inc(s["z_mm"], 1)
                if live(1):
                    after(pe, "p0T_done", b_)
                    for h in range(A):
                        last = mm(ps[:, B_PV0, h * (E + 1):(h + 1) * (E + 1)], p0T[:, i1, h, :], hp[:, i1, h, :],
                                  start=True, stop=True)
                    last.then_inc(s["pv0_mm"], 1)
            steps(pe, body)


def kernel(x, adj, L0_gnn_W, L0_gnn_b, L0_gnn_w_src, L0_gnn_w_dst, L0_gnn_H_w, L0_gnn_H_b, L1_gnn_Wq, L1_gnn_bq,
           L1_gnn_Wk, L1_gnn_bk, L1_gnn_Wv, L1_gnn_bv, L1_gnn_Wf, L1_gnn_bf):
    import numpy as np
    import concourse.bacc as bacc
    from concourse import mybir as mb
    from concourse.bass_utils import run_bass_kernel_spmd

    def rows(w):
        return np.ascontiguousarray(np.asarray(w).reshape(3, 128, -1).transpose(1, 0, 2))

    def cols(v):
        return np.ascontiguousarray(np.asarray(v).reshape(3, 128).T)

    W = np.asarray(L0_gnn_W)
    arrays = {
        "x": np.asarray(x), "adj": np.asarray(adj),
        "W": np.ascontiguousarray(W.reshape(12, 3, 128, 32).transpose(2, 1, 0, 3)),
        "b": np.asarray(L0_gnn_b), "w_src": cols(L0_gnn_w_src), "w_dst": cols(L0_gnn_w_dst),
        "HwT": rows(np.asarray(L0_gnn_H_w).T), "H_b": np.asarray(L0_gnn_H_b),
        "Wq": rows(L1_gnn_Wq), "bq": cols(L1_gnn_bq), "Wk": rows(L1_gnn_Wk), "bk": cols(L1_gnn_bk),
        "Wv": rows(L1_gnn_Wv), "bv": np.asarray(L1_gnn_bv), "Wf": rows(L1_gnn_Wf), "bf": np.asarray(L1_gnn_bf),
    }
    nc = bacc.Bacc("TRN2", target_bir_lowering=False, num_devices=1)
    drams = {}
    for name, v in arrays.items():
        drams[name] = nc.dram_tensor(f"in_{name}", v.shape, mb.dt.from_np(v.dtype), kind="ExternalInput").ap()
    shape = arrays["x"].shape
    out = nc.dram_tensor("out_x", shape, mb.dt.float32, kind="ExternalOutput").ap()
    program(nc, out=out, **drams)
    r = run_bass_kernel_spmd(nc, [{f"in_{k}": v for k, v in arrays.items()}], core_ids=[0])
    return r.results[0]["out_x"]
```

```python
from contextlib import ExitStack

import concourse.bass as bass
from concourse import mybir

ALU = mybir.AluOpType
ACT = mybir.ActivationFunctionType
AX_X = mybir.AxisListType.X
F32 = mybir.dt.float32
BF16 = mybir.dt.bfloat16
F16 = mybir.dt.float16
I32 = mybir.dt.int32
RMAX = bass.bass_isa.ReduceOp.max
U8 = mybir.dt.uint8

P = 128
UNROLL = 4
EPS = 1e-5
MASKED0 = -999.0
NEG = -9e15
SLOPE = 0.2
HS = 1024.0
W_TOP, V_TOP = 2.0 ** 13, 2.0 ** 5
W_H, W_G, W_Q, W_K, W_V, W_F, V0, V1, M_GB = range(9)


def program(nc, x, adj, W, b, w_src, w_dst, HwT, H_b, Wq, bq, Wk, bk, Wv, bv, Wf, bf, out):
    NB, N, D = x.shape
    E = b.shape[0]
    A = D // E
    HEADS = 6
    DH = D // HEADS
    KC = D // P
    HP = P // DH
    AB = 512 // N
    assert N == P and KC == 3 and A == 12 and E == 32 and HP == 2 and NB % UNROLL == 0
    SCALE = float(DH) ** -0.5

    with ExitStack() as ctx:
        def sb(name, shape, dt=F32):
            return ctx.enter_context(nc.sbuf_tensor(name, shape, dt))

        def sem(name):
            return ctx.enter_context(nc.semaphore(name))

        ident = sb("ident", [P, P])
        identb = sb("identb", [P, P], BF16)
        whi = sb("whi", [P, 6, KC, D], F16)
        wlo = sb("wlo", [P, 6, KC, D], F16)
        wmax = sb("wmax", [P, 9])
        wall = sb("wall", [P, 9])
        scl = sb("scl", [P, 8])
        inv = sb("inv", [P, 8])
        fac = sb("fac", [P, 8])
        qkb = sb("qkb", [P, 2, KC])
        bvr = sb("bvr", [P, D])
        bfr = sb("bfr", [P, D])
        b0r = sb("b0r", [P, E])
        w_ds = sb("w_ds", [P, 2, D])
        sel_d = sb("sel_d", [96, A, P], BF16)
        one_s = sb("one_s", [96, A, P], BF16)
        sel_b = sb("sel_b", [96, P], BF16)
        hb = sb("hb", [96, D])
        hbp = sb("hbp", [96, D], BF16)
        hbr = sb("hbr", [96, D])
        hbm = sb("hbm", [96, D], BF16)
        mhalf = sb("mhalf", [P, 1])

        xin = sb("xin", [P, 4, D])
        adj8 = sb("adj8", [P, 4, N], U8)
        maskb = sb("maskb", [P, 4, N], BF16)
        h0 = sb("h0", [P, 4, D])
        xh = sb("xh", [P, 2, D])
        tg = sb("tg", [P, 2, D])
        sg = sb("sg", [P, 2, D])
        hq = sb("hq", [P, 2, D])
        c0 = sb("c0", [P, 2, D])
        h0T = sb("h0T", [P, 2, 2, KC, N], F16)
        th = sb("th", [P, 2, D])
        ths = sb("ths", [P, 2, D])
        hp = sb("hp", [P, 2, A, E + 1])
        sd32 = sb("sd32", [P, 2 * A])
        sdn = sb("sdn", [P, 2, 3, 32], BF16)
        sdp = sb("sdp", [96, 2, N], BF16)
        u2 = sb("u2", [P, 2, A, N])
        lk = sb("lk", [P, 2, A, N])
        p0 = sb("p0", [P, 2, A, N])
        p0T = sb("p0T", [P, 2, A, N])
        mx0 = sb("mx0", [P, 2, A])
        rd0 = sb("rd0", [P, 2, A])
        feat = sb("feat", [P, 2, D])
        fneg = sb("fneg", [P, 2, D])
        fexp = sb("fexp", [P, 2, D])
        fg = sb("fg", [P, 2, D])
        eg = sb("eg", [P, 2, D])
        x1 = sb("x1", [P, 2, D])
        x1b = sb("x1b", [P, 2, D])
        h1 = sb("h1", [P, 2, D])
        h1T = sb("h1T", [P, 2, 2, KC, N], F16)
        qkT = sb("qkT", [P, 2, 2, KC, N])
        vp = sb("vp", [P, 2, HEADS, DH + 1])
        p1 = sb("p1", [P, 2, HP, KC, N])
        p1T = sb("p1T", [P, 2, HP, KC, N])
        mx1 = sb("mx1", [P, 2, HP, KC])
        mxn = sb("mxn", [P, 2, HP, KC])
        rd1 = sb("rd1", [P, 2, HEADS])
        cx = sb("cx", [P, 2, D])
        cxT = sb("cxT", [P, 2, 2, KC, N], F16)
        res = sb("res", [P, 2, D])
        bst = [sb(f"bst{i}", [P, 2, 6]) for i in range(2)]
        mv = [sb(f"mv{i}", [P, 2, 2]) for i in range(2)]
        ve = [sb(f"ve{i}", [P, 2, 1]) for i in range(2)]
        rstd = [sb(f"rstd{i}", [P, 2, 1]) for i in range(2)]
        nmr = [sb(f"nmr{i}", [P, 2, 1]) for i in range(2)]

        ps = ctx.enter_context(nc.psum_tensor("ps", [P, 8, 512], F32))

        def bank(i, n=N, k=KC):
            return ps[:, i, 0:k * n].rearrange("p (c n) -> p c n", n=n)

        B_H0T, B_GATE, B_H, B_SD, B_CTXT, B_OUT, B_PV1, B_PV0, B_H1T, B_V = 4, 4, 6, 3, 2, 0, 5, 5, 3, 7
        B_P1T, B_QK, B_P0T, B_SC = 0, 1, 4, 0
        Z_BANKS = (2, 3, 7)

        def w32(m):
            return (u2, p0, p0T)[m // 2][:, m % 2, 0:KC * D // N, :].rearrange("p a n -> p (a n)").rearrange(
                "p (c n) -> p c n", n=D)

        sdT_bank = ps[0:96, B_SD, 0:N // 2].bitcast(BF16)

        w_loaded = [sem(f"w_loaded{i}") for i in range(14)]
        setup_pool = sem("setup_pool")
        setup_dve = sem("setup_dve")
        maxima_done = sem("maxima_done")
        maxima_spread = sem("maxima_spread")
        scales_done = sem("scales_done")
        weights_done = sem("weights_done")
        x_loaded = [sem(f"x_loaded{i}") for i in range(4)]
        adj_loaded = [sem(f"adj_loaded{i}") for i in range(4)]
        stored = [sem(f"stored{i}") for i in range(2)]
        names = """bn0_done aggr0_done ve0_done rstd0_done nmr0_done h0_done xh_done mask_done
            h0T_mm h0T_done H_mm th_done hp_done gate_mm tg_done ths_done sd32_done sdhi_done sdr1_done
            sdmid_done sdlo_done sdT_mm sd_done h0Th_done h1Th_done cxTh_done z_mm u2a_done u2_done lka_done lk_done mx0a_done mx0_done sub0a_done sub0_done p0a_done p0_done
            p0Ta_mm p0T_mm p0Ta_done p0T_done pv0_mm rd0_done feat_done fneg_done fexp_done fg_done fc_done eg_done x1_done sg_done hq_done hg_done c0_done
            bn1_done aggr1_done ve1_done rstd1_done nmr1_done h1_done x1b_done h1T_mm h1T_done qk_mm qk_done
            v_mm v_done sc_mm mx1_done mxn_done p1_done p1T_mm p1T_done pv1_mm rd1_done cx_done cxT_mm cxT_done
            out_mm res_done""".split()
        s = {n: sem(n) for n in names}

        def after(eng, name, g):
            if not isinstance(g, int) or 0 <= g < NB:
                eng.wait_ge(s[name], g + 1)

        def steps(eng, body):
            def fixed(t):
                body(t, t % UNROLL, t // UNROLL, lambda k: 0 <= t - k < NB)
            for t in range(-1, 2 * UNROLL):
                fixed(t)
            with eng.Fori(2, NB // UNROLL - 1) as turn:
                for j in range(UNROLL):
                    body(turn * UNROLL + j, j, turn, lambda k: True)
            for t in range(NB - UNROLL, NB + 3):
                fixed(t)

        block = ctx.enter_context(nc.Block())

        @block.sync
        def _(sp):
            def load(g, slot):
                sp.dma_start(xin[:, slot, :], x[g]).then_inc(x_loaded[slot], 16)
                sp.dma_start(adj8[:, slot, :], adj[g]).then_inc(adj_loaded[slot], 16)
            def on_rows(v, rows):
                return v.rearrange("(o n) -> o n", o=1).to_broadcast([rows, v.shape[0]])
            load(0, 0)
            for n, (dst, src) in enumerate([
                    (w32(W_H), W), (w32(W_G), HwT), (w32(W_Q), Wq), (w32(W_K), Wk), (w32(W_V), Wv), (w32(W_F), Wf), (hb[:], on_rows(H_b, 96)), (b0r[:], on_rows(b, P)), (bvr[:], on_rows(bv, P)),
                    (w_ds[:, 0, :], on_rows(w_dst, P)), (w_ds[:, 1, :], on_rows(w_src, P)),
                    (qkb[:, 0, :], bq), (qkb[:, 1, :], bk), (bfr[:], on_rows(bf, P))]):
                sp.dma_start(dst, src).then_inc(w_loaded[n], 16)
            load(1, 1)

            def body(t, j, turn, live):
                if live(-2):
                    after(sp, "xh_done", t - 2)
                    after(sp, "mask_done", t - 2)
                    load(t + 2, (j + 2) % 4)
                if live(3):
                    after(sp, "res_done", t - 3)
                    sp.dma_start(out[t - 3], res[:, (j - 3) % 2, :]).then_inc(stored[(j - 3) % 2], 16)
            steps(sp, lambda t, j, turn, live: None if isinstance(t, int) and t < 0 else body(t, j, turn, live))
            for i in range(2):
                sp.wait_ge(stored[i], 16 * (NB // 2))

        @block.gpsimd
        def _(pool):
            for n, m in enumerate((ident, identb, sel_d, one_s, sel_b)):
                nc.gpsimd.memset(m[:], 0.0).then_inc(setup_pool, 1)
            nc.gpsimd.memset(mhalf[:], -0.5).then_inc(setup_pool, 1)
            nc.gpsimd.memset(hp[:], 1.0).then_inc(setup_pool, 1)
            nc.gpsimd.memset(vp[:], 1.0).then_inc(setup_pool, 1)
            pool.wait_ge(setup_pool, 8)
            count = 8
            for m in (ident, identb):
                nc.gpsimd.affine_select(out=m[:], in_=m[:], compare_op=ALU.not_equal, fill=1.0, base=0,
                                        pattern=[[-1, P]], channel_multiplier=1).then_inc(setup_pool, 1)
                count += 1
            for r in range(3):
                for m, first in ((sel_d, 0), (one_s, A)):
                    nc.gpsimd.affine_select(out=m[:], in_=m[:], compare_op=ALU.not_equal, fill=1.0,
                                            base=-(32 * r + first), pattern=[[-1, A], [0, P]],
                                            channel_multiplier=1).then_inc(setup_pool, 1)
                    count += 1
                    pool.wait_ge(setup_pool, count)
                nc.gpsimd.affine_select(out=sel_b[:], in_=sel_b[:], compare_op=ALU.not_equal, fill=1.0,
                                        base=-32 * r, pattern=[[0, P]], channel_multiplier=1).then_inc(setup_pool, 1)
                count += 1
                pool.wait_ge(setup_pool, count)
            nc.gpsimd.memset(sdn[:], 0.0).then_inc(setup_pool, 1)
            pool.wait_ge(maxima_done, 1)
            nc.gpsimd.partition_all_reduce(wall[:], wmax[:], P, RMAX).then_inc(maxima_spread, 1)
            for n in (9, 10, 13):
                pool.wait_ge(w_loaded[n], 16)

            def body(t, j, turn, live):
                if live(1):
                    after(pool, "tg_done", t - 1)
                if live(0):
                    after(pool, "h0_done", t)
                    nc.gpsimd.tensor_tensor(xh[:, j % 2, :], xin[:, j, :], h0[:, j, :], ALU.add).then_inc(s["xh_done"], 1)
                if live(1):
                    g, i, k = t - 1, (j - 1) % 2, (j - 1) % 4
                    nc.gpsimd.tensor_scalar(sg[:, i, :], tg[:, i, :], 1.0, 0.5, ALU.add, ALU.mult).then_inc(s["sg_done"], 1)
                    nc.gpsimd.tensor_scalar(hq[:, i, :], h0[:, k, :], 1.0, 1.0, ALU.add, ALU.mult).then_inc(s["hq_done"], 1)
                    after(pool, "sg_done", g)
                    after(pool, "hq_done", g)
                    nc.gpsimd.tensor_tensor(hq[:, i, :], hq[:, i, :], sg[:, i, :], ALU.mult).then_inc(s["hg_done"], 1)
                    after(pool, "hg_done", g)
                    nc.gpsimd.tensor_tensor(c0[:, i, :], xh[:, i, :], hq[:, i, :], ALU.subtract).then_inc(s["c0_done"], 1)
                if live(2):
                    g, i = t - 2, (j - 2) % 2
                    after(pool, "ve1_done", g)
                    nc.gpsimd.tensor_tensor(rstd[1][:, i, :], ve[1][:, i, :], mhalf[:], ALU.pow).then_inc(s["rstd1_done"], 1)
                if live(0):
                    after(pool, "th_done", t)
                    after(pool, "sd32_done", t - 1)
                    nc.gpsimd.tensor_tensor(ths[:], th[:, j % 2, :].unsqueeze(1).to_broadcast([P, 2, D]), w_ds[:],
                                            ALU.mult).then_inc(s["ths_done"], 1)
                if live(1):
                    g, i = t - 1, (j - 1) % 2
                    for part, heads in (("a", slice(0, 2 * AB)), ("", slice(2 * AB, A))):
                        after(pool, f"mx0{part}_done", g)
                        nc.gpsimd.tensor_tensor(lk[:, i, heads, :], lk[:, i, heads, :],
                                                mx0[:, i, heads].unsqueeze(2).to_broadcast([P, heads.stop - heads.start, N]),
                                                ALU.subtract).then_inc(s[f"sub0{part}_done"], 1)
                if live(-1):
                    g, i, k = t + 1, (j + 1) % 2, (j + 1) % 4
                    pool.wait_ge(adj_loaded[k], 16 * (turn + (1 if j == 3 else 0)) + 16)
                    after(pool, "sc_mm", g - 4)
                    after(pool, "ve0_done", g)
                    nc.gpsimd.tensor_tensor(rstd[0][:, i, :], ve[0][:, i, :], mhalf[:], ALU.pow).then_inc(s["rstd0_done"], 1)
                    nc.gpsimd.tensor_scalar(maskb[:, k, :], adj8[:, k, :], -1.0, -NEG, ALU.add,
                                            ALU.mult).then_inc(s["mask_done"], 1)
                if live(2):
                    g, i = t - 2, (j - 2) % 2
                    after(pool, "x1_done", g)
                    after(pool, "res_done", g - 2)
                    nc.gpsimd.tensor_tensor(x1b[:, i, :], x1[:, i, :], bfr[:], ALU.add).then_inc(s["x1b_done"], 1)
            steps(pool, body)

        @block.scalar
        def _(act):
            act.wait_ge(scales_done, 1)
            act.wait_ge(weights_done, 1)

            def body(t, j, turn, live):
                a, b_, c, d = t, t - 1, t - 2, t - 3
                i0, i1 = j % 2, (j + 1) % 2
                if live(2):
                    after(act, "fneg_done", c)
                    nc.scalar.activation(fexp[:, i0, :], fneg[:, i0, :], ACT.Exp).then_inc(s["fexp_done"], 1)
                if live(1):
                    after(act, "z_mm", b_)
                    after(act, "lk_done", b_ - 2)
                    after(act, "lka_done", b_ - 2)
                    nc.scalar.mul(u2[:, i1, 2 * AB:A, :], bank(Z_BANKS[2], k=AB), SLOPE).then_inc(s["u2_done"], 1)
                    nc.scalar.mul(u2[:, i1, 0:2 * AB, :],
                                  ps[:, Z_BANKS[0]:Z_BANKS[0] + 2, :].rearrange("p b (c n) -> p (b c) n", n=N),
                                  SLOPE).then_inc(s["u2a_done"], 1)
                if live(3):
                    after(act, "p1T_mm", d)
                    nc.scalar.copy(p1T[:, i1, :, :, :],
                                   ps[:, B_P1T:B_P1T + 2, 0:KC * N].rearrange("p b (c n) -> p b c n", n=N)
                                   ).then_inc(s["p1T_done"], 1)
                if live(0):
                    after(act, "H_mm", a)
                    after(act, "ths_done", a - 2)
                    nc.scalar.activation(th[:, i0, :], ps[:, B_H, 0:D], ACT.Tanh,
                                         scale=inv[:, W_H:W_H + 1]).then_inc(s["th_done"], 1)
                if live(2):
                    after(act, "nmr1_done", c)
                    after(act, "h1T_mm", c - 2)
                    nc.scalar.activation(h1[:, i0, :], x1[:, i0, :], ACT.Relu, bias=nmr[1][:, i0, :],
                                         scale=rstd[1][:, i0, :]).then_inc(s["h1_done"], 1)
                if live(0):
                    after(act, "gate_mm", a)
                    after(act, "sg_done", a - 2)
                    nc.scalar.activation(tg[:, i0, :], ps[:, B_GATE, 0:D], ACT.Tanh,
                                         scale=fac[:, W_G:W_G + 1]).then_inc(s["tg_done"], 1)
                if live(2):
                    after(act, "h1T_mm", c)
                    nc.scalar.mul(h1T[:, i0, 0], bank(B_H1T), HS).then_inc(s["h1Th_done"], 1)
                if live(3):
                    after(act, "cxT_mm", d)
                    nc.scalar.copy(cxT[:, i1, 0], bank(B_CTXT)).then_inc(s["cxTh_done"], 1)
                if live(1):
                    after(act, "p0T_mm", b_ - 2)
                    for part, heads in (("a", slice(0, 2 * AB)), ("", slice(2 * AB, A))):
                        after(act, f"sub0{part}_done", b_)
                        nc.scalar.activation(p0[:, i1, heads, :], lk[:, i1, heads, :], ACT.Exp).then_inc(s[f"p0{part}_done"], 1)
                if live(-1):
                    after(act, "nmr0_done", t + 1)
                    after(act, "hq_done", t - 3)
                    after(act, "xh_done", t - 3)
                    nc.scalar.activation(h0[:, (j + 1) % 4, :], xin[:, (j + 1) % 4, :], ACT.Relu,
                                         bias=nmr[0][:, i1, :], scale=rstd[0][:, i1, :]).then_inc(s["h0_done"], 1)
                if live(0):
                    after(act, "sdT_mm", a)
                    after(act, "z_mm", a - 2)
                    nc.scalar.copy(sdp[:, i0, :], sdT_bank).then_inc(s["sd_done"], 1)
                if live(1):
                    after(act, "p0Ta_mm", b_)
                    nc.scalar.copy(p0T[:, i1, 0:2 * AB, :],
                                   ps[:, B_P0T:B_P0T + 2, :].rearrange("p b (c n) -> p (b c) n", n=N)
                                   ).then_inc(s["p0Ta_done"], 1)
                    after(act, "p0T_mm", b_)
                    nc.scalar.copy(p0T[:, i1, 2 * AB:A, :], bank(B_P0T + 2, k=AB)).then_inc(s["p0T_done"], 1)
                if live(2):
                    after(act, "mxn_done", c)
                    after(act, "p1T_mm", c - 2)
                    for h in range(HEADS):
                        n, m = h % 2, h // 2
                        last = nc.scalar.activation(p1[:, i0, n, m, :], bank(B_SC + n)[:, m, :], ACT.Exp,
                                                    bias=mxn[:, i0, n, m:m + 1], scale=SCALE)
                    last.then_inc(s["p1_done"], 1)
                if live(-1):
                    after(act, "h0T_mm", t + 1)
                    nc.scalar.mul(h0T[:, i1, 0], bank(B_H0T), HS).then_inc(s["h0Th_done"], 1)
            steps(act, body)

        @block.vector
        def _(dve):
            count = 0

            def chain(instruction):
                nonlocal count
                count += 1
                instruction.then_inc(setup_dve, 1)
                dve.wait_ge(setup_dve, count)

            ts, tt, stt = nc.vector.tensor_scalar, nc.vector.tensor_tensor, nc.vector.scalar_tensor_tensor
            chain(nc.vector.memset(wmax[:], 0.0))
            for n, (col, src) in enumerate([(m, w32(m).rearrange("p c n -> p (c n)")) for m in range(6)]
                                           + [(M_GB, hb[:]), (V0, b0r[:]), (V1, bvr[:])]):
                dve.wait_ge(w_loaded[n], 16)
                last = nc.vector.tensor_reduce(wmax[0:src.shape[0], col:col + 1], src, AX_X, ALU.max,
                                               apply_absolute_value=True)
            last.then_inc(maxima_done, 1)
            dve.wait_ge(maxima_spread, 1)
            for dst, src in ((V0, W_H), (V1, W_V), (W_G, M_GB), (W_Q, W_K)):
                chain(tt(wall[:, dst:dst + 1], wall[:, dst:dst + 1], wall[:, src:src + 1], ALU.max))
            chain(nc.vector.tensor_copy(wall[:, W_K:W_K + 1], wall[:, W_Q:W_Q + 1]))
            chain(ts(wall[:], wall[:], 1e-30, None, ALU.max))
            chain(ts(wall[:].bitcast(I32), wall[:].bitcast(I32), 0x7F800000, None, ALU.bitwise_and))
            chain(nc.vector.reciprocal(scl[:], wall[:, 0:8]))
            chain(ts(scl[:, 0:6], scl[:, 0:6], W_TOP, None, ALU.mult))
            chain(ts(scl[:, 6:8], scl[:, 6:8], V_TOP, None, ALU.mult))
            chain(ts(inv[:, 0:6], wall[:, 0:6], 1.0 / (W_TOP * HS), None, ALU.mult))
            chain(ts(inv[:, 6:8], wall[:, 6:8], 1.0 / V_TOP, None, ALU.mult))
            for dst, f, other in ((W_H, inv, scl[:, V0:V0 + 1]), (W_V, inv, scl[:, V1:V1 + 1])):
                chain(tt(fac[:, dst:dst + 1], f[:, dst:dst + 1], other, ALU.mult))
            chain(stt(fac[:, W_F:W_F + 1], inv[:, W_F:W_F + 1], HS, inv[:, V1:V1 + 1], ALU.mult, ALU.mult))
            chain(ts(fac[:, W_G:W_G + 1], inv[:, W_G:W_G + 1], 0.5, None, ALU.mult))
            chain(ts(b0r[:], b0r[:], scl[:, V0:V0 + 1], None, ALU.mult))
            chain(ts(bvr[:], bvr[:], scl[:, V1:V1 + 1], None, ALU.mult))
            for n in (11, 12):
                dve.wait_ge(w_loaded[n], 16)
            dve.wait_ge(setup_pool, 20)
            chain(ts(hb[:], hb[:], scl[0:96, W_G:W_G + 1], HS, ALU.mult, ALU.mult))
            nc.vector.tensor_copy(hbp[:], hb[:]).then_inc(scales_done, 1)
            dve.wait_ge(scales_done, 1)
            chain(tt(hbr[:], hb[:], hbp[:], ALU.subtract))
            chain(nc.vector.tensor_copy(hbm[64:96], hbr[64:96]))
            chain(nc.vector.tensor_copy(hbp[32:64], hbr[32:64]))
            chain(tt(hbp[64:96], hbr[64:96], hbm[64:96], ALU.subtract))
            for m in range(6):
                chain(ts(whi[:, m], w32(m), scl[:, m:m + 1], None, ALU.mult))
                last = stt(wlo[:, m], w32(m), scl[:, m:m + 1], whi[:, m], ALU.mult, ALU.subtract)
            last.then_inc(weights_done, 1)

            def norm(k, src, g, i, between):
                nc.vector.bn_stats(bst[k][:, i, :], src).then_inc(s[f"bn{k}_done"], 1)
                after(dve, f"bn{k}_done", g)
                between()
                nc.vector.bn_aggr(mv[k][:, i, :], bst[k][:, i, :]).then_inc(s[f"aggr{k}_done"], 1)
                after(dve, f"aggr{k}_done", g)
                nc.vector.tensor_scalar(ve[k][:, i, :], mv[k][:, i, 1:2], EPS, None, ALU.add).then_inc(s[f"ve{k}_done"], 1)

            def norm_bias(k, g, i):
                after(dve, f"rstd{k}_done", g)
                nc.vector.scalar_tensor_tensor(nmr[k][:, i, :], mv[k][:, i, 0:1], -1.0, rstd[k][:, i, :],
                                               ALU.mult, ALU.mult).then_inc(s[f"nmr{k}_done"], 1)

            def low_part(name, xT, bank_, scale, g):
                after(dve, f"{name}h_done", g)
                nc.vector.scalar_tensor_tensor(xT[:, 1], bank(bank_), scale, xT[:, 0], ALU.mult,
                                               ALU.subtract).then_inc(s[f"{name}_done"], 1)

            pv1 = ps[:, B_PV1, 0:HEADS * (DH + 1)].rearrange("p (h e) -> p h e", e=DH + 1)

            def body(t, j, turn, live):
                a, b_, c, d = t, t - 1, t - 2, t - 3
                i0, i1 = j % 2, (j + 1) % 2
                if live(2):
                    pv = ps[:, B_PV0, 0:A * (E + 1)].rearrange("p (a e) -> p a e", e=E + 1)
                    after(dve, "pv0_mm", c)
                    nc.vector.reciprocal(rd0[:, i0, :], pv[:, :, E:E + 1]).then_inc(s["rd0_done"], 1)
                    after(dve, "rd0_done", c)
                    nc.vector.scalar_tensor_tensor(feat[:, i0, :].rearrange("p (a e) -> p a e", e=E), pv[:, :, 0:E],
                                                   inv[:, V0:V0 + 1], rd0[:, i0, :].unsqueeze(2).to_broadcast([P, A, E]),
                                                   ALU.mult, ALU.mult).then_inc(s["feat_done"], 1)
                    after(dve, "feat_done", c)
                    nc.vector.tensor_scalar(fneg[:, i0, :], feat[:, i0, :], 0.0, None, ALU.min).then_inc(s["fneg_done"], 1)
                if live(0):
                    low_part("h0T", h0T[:, i0], B_H0T, HS, a)
                if live(2):
                    after(dve, "c0_done", c)
                    nc.vector.scalar_tensor_tensor(fg[:, i0, :], feat[:, i0, :], 0.0, sg[:, i0, :], ALU.max,
                                                   ALU.mult).then_inc(s["fg_done"], 1)
                    after(dve, "fg_done", c)
                    nc.vector.tensor_tensor(fg[:, i0, :], fg[:, i0, :], c0[:, i0, :], ALU.add).then_inc(s["fc_done"], 1)
                    after(dve, "fexp_done", c)
                    nc.vector.tensor_tensor(eg[:, i0, :], fexp[:, i0, :], sg[:, i0, :], ALU.mult).then_inc(s["eg_done"], 1)
                    after(dve, "eg_done", c)
                    after(dve, "fc_done", c)
                    after(dve, "x1b_done", c - 2)
                    after(dve, "h1_done", c - 2)
                    nc.vector.tensor_tensor(x1[:, i0, :], eg[:, i0, :], fg[:, i0, :], ALU.add).then_inc(s["x1_done"], 1)
                def leaky_last():
                    if live(1):
                        after(dve, "u2_done", b_)
                        after(dve, "p0_done", b_ - 2)
                        nc.vector.scalar_tensor_tensor(lk[:, i1, 2 * AB:A, :], bank(Z_BANKS[2], k=AB), MASKED0,
                                                       u2[:, i1, 2 * AB:A, :], ALU.max, ALU.max).then_inc(s["lk_done"], 1)
                if live(2):
                    after(dve, "x1_done", c)
                    norm(1, x1[:, i0, :], c, i0, leaky_last)
                else:
                    leaky_last()
                if live(1):
                    after(dve, "u2a_done", b_)
                    after(dve, "p0_done", b_ - 2)
                    nc.vector.scalar_tensor_tensor(
                        lk[:, i1, 0:2 * AB, :],
                        ps[:, Z_BANKS[0]:Z_BANKS[0] + 2, :].rearrange("p b (c n) -> p (b c) n", n=N), MASKED0,
                        u2[:, i1, 0:2 * AB, :], ALU.max, ALU.max).then_inc(s["lka_done"], 1)
                if live(2):
                    norm_bias(1, c, i0)
                if live(3):
                    after(dve, "pv1_mm", d)
                    nc.vector.reciprocal(rd1[:, i1, :], pv1[:, :, DH:DH + 1]).then_inc(s["rd1_done"], 1)
                    after(dve, "rd1_done", d)
                    nc.vector.tensor_tensor(cx[:, i1, :].rearrange("p (h e) -> p h e", e=DH), pv1[:, :, 0:DH],
                                            rd1[:, i1, :].unsqueeze(2).to_broadcast([P, HEADS, DH]),
                                            ALU.mult).then_inc(s["cx_done"], 1)
                if live(1):
                    after(dve, "lka_done", b_)
                    nc.vector.tensor_reduce(mx0[:, i1, 0:2 * AB], lk[:, i1, 0:2 * AB, :], AX_X, ALU.max).then_inc(s["mx0a_done"], 1)
                if live(2):
                    low_part("h1T", h1T[:, i0], B_H1T, HS, c)
                if live(3):
                    low_part("cxT", cxT[:, i1], B_CTXT, 1.0, d)
                if live(1):
                    after(dve, "lk_done", b_)
                    nc.vector.tensor_reduce(mx0[:, i1, 2 * AB:A], lk[:, i1, 2 * AB:A, :], AX_X, ALU.max).then_inc(s["mx0_done"], 1)
                def values():
                    if live(0):
                        after(dve, "th_done", a)
                        nc.vector.scalar_tensor_tensor(hp[:, i0, :, 0:E], ps[:, B_H, 0:D].rearrange("p (a e) -> p a e", e=E),
                                                       fac[:, W_H:W_H + 1], b0r[:].unsqueeze(1).to_broadcast([P, A, E]),
                                                       ALU.mult, ALU.add).then_inc(s["hp_done"], 1)
                if live(-1):
                    k = (j + 1) % 4
                    dve.wait_ge(x_loaded[k], 16 * (turn + (1 if j == 3 else 0)) + 16)
                    norm(0, xin[:, k, :], t + 1, i1, values)
                else:
                    values()
                if live(-1):
                    norm_bias(0, t + 1, i1)
                if live(0):
                    hi, mid, lo = (sdn[:, i0, r, 0:2 * A] for r in range(3))
                    after(dve, "ths_done", a)
                    nc.vector.tensor_reduce(sd32[:], ths[:].rearrange("p k (a e) -> p (k a) e", e=E), AX_X,
                                            ALU.add).then_inc(s["sd32_done"], 1)
                    after(dve, "sd32_done", a)
                    after(dve, "sdT_mm", a - 2)
                    nc.vector.tensor_copy(hi, sd32[:]).then_inc(s["sdhi_done"], 1)
                    after(dve, "sdhi_done", a)
                    nc.vector.tensor_tensor(sd32[:], sd32[:], hi, ALU.subtract).then_inc(s["sdr1_done"], 1)
                    after(dve, "sdr1_done", a)
                    nc.vector.tensor_copy(mid, sd32[:]).then_inc(s["sdmid_done"], 1)
                    after(dve, "sdmid_done", a)
                    nc.vector.tensor_tensor(lo, sd32[:], mid, ALU.subtract).then_inc(s["sdlo_done"], 1)
                if live(2):
                    after(dve, "v_mm", c)
                    nc.vector.scalar_tensor_tensor(vp[:, i0, :, 0:DH], ps[:, B_V, 0:D].rearrange("p (h e) -> p h e", e=DH),
                                                   fac[:, W_V:W_V + 1], bvr[:].rearrange("p (h e) -> p h e", e=DH),
                                                   ALU.mult, ALU.add).then_inc(s["v_done"], 1)
                if live(3):
                    after(dve, "out_mm", d)
                    after(dve, "x1b_done", d)
                    if not isinstance(d, int) or d >= 2:
                        dve.wait_ge(stored[i1], 32 * turn + 16 * ((j - 3) // 2))
                    nc.vector.scalar_tensor_tensor(res[:, i1, :], ps[:, B_OUT, 0:D], fac[:, W_F:W_F + 1], x1b[:, i1, :],
                                                   ALU.mult, ALU.add).then_inc(s["res_done"], 1)
                if live(2):
                    after(dve, "qk_mm", c)
                    nc.vector.scalar_tensor_tensor(qkT[:, i0, :, :, :],
                                                   ps[:, B_QK:B_QK + 2, 0:KC * N].rearrange("p b (c n) -> p b c n", n=N),
                                                   inv[:, W_Q:W_Q + 1], qkb[:].unsqueeze(3).to_broadcast([P, 2, KC, N]),
                                                   ALU.mult, ALU.add).then_inc(s["qk_done"], 1)
                if live(2):
                    scores = ps[:, B_SC:B_SC + 2, 0:KC * N].rearrange("p b (c n) -> p b c n", n=N)
                    after(dve, "sc_mm", c)
                    nc.vector.tensor_reduce(mx1[:, i0, :, :], scores, AX_X, ALU.max).then_inc(s["mx1_done"], 1)
                    after(dve, "mx1_done", c)
                    nc.vector.tensor_scalar(mxn[:, i0, :, :], mx1[:, i0, :, :], -SCALE, None, ALU.mult).then_inc(s["mxn_done"], 1)
            steps(dve, body)

        @block.tensor
        def _(pe):
            mm = nc.tensor.matmul
            pe.wait_ge(setup_pool, 19)
            pe.wait_ge(weights_done, 1)

            def transposes(dst, src):
                for c in range(KC):
                    last = nc.tensor.transpose(dst[:, c, :], src[:, c * P:(c + 1) * P], ident[:])
                return last

            def project(dst, name, xT, w, g, start=True):
                after(pe, f"{name}h_done", g)
                for c in range(KC):
                    for n, part in enumerate((whi, wlo)):
                        mm(dst, xT[:, 0, c, :], part[:, w, c, :], start=(start and c == 0 and n == 0), stop=False)
                after(pe, f"{name}_done", g)
                for c in range(KC):
                    last = mm(dst, xT[:, 1, c, :], whi[:, w, c, :], start=False, stop=(c == KC - 1))
                return last

            def body(t, j, turn, live):
                a, b_, c, d = t, t - 1, t - 2, t - 3
                i0, i1 = j % 2, (j + 1) % 2
                if live(3):
                    after(pe, "p1_done", d)
                    for h in range(HEADS):
                        last = nc.tensor.transpose(bank(B_P1T + h % 2)[:, h // 2, :], p1[:, i1, h % 2, h // 2, :], ident[:])
                    last.then_inc(s["p1T_mm"], 1)
                if live(0):
                    project(ps[:, B_H, 0:D], "h0T", h0T[:, i0], W_H, a).then_inc(s["H_mm"], 1)
                if live(3):
                    after(pe, "p1T_done", d)
                    after(pe, "feat_done", c)
                    for h in range(HEADS):
                        last = mm(ps[:, B_PV1, h * (DH + 1):(h + 1) * (DH + 1)], p1T[:, i1, h % 2, h // 2, :],
                                  vp[:, i1, h, :], start=True, stop=True)
                    last.then_inc(s["pv1_mm"], 1)
                if live(0):
                    mm(ps[:, B_GATE, 0:D], sel_b[:], hbp[:], start=True, stop=False)
                    project(ps[:, B_GATE, 0:D], "h0T", h0T[:, i0], W_G, a, start=False).then_inc(s["gate_mm"], 1)
                if live(2):
                    after(pe, "h1_done", c)
                    after(pe, "lka_done", t - 1)
                    transposes(bank(B_H1T), h1[:, i0, :]).then_inc(s["h1T_mm"], 1)
                if live(3):
                    after(pe, "cx_done", d)
                    after(pe, "lka_done", t - 1)
                    transposes(bank(B_CTXT), cx[:, i1, :]).then_inc(s["cxT_mm"], 1)
                if live(2):
                    after(pe, "lk_done", t - 1)
                    project(ps[:, B_V, 0:D], "h1T", h1T[:, i0], W_V, c).then_inc(s["v_mm"], 1)
                if live(3):
                    project(ps[:, B_OUT, 0:D], "cxT", cxT[:, i1], W_F, d).then_inc(s["out_mm"], 1)
                if live(2):
                    for n, w in enumerate((W_Q, W_K)):
                        for m in range(KC):
                            terms = [(part, x, k) for part, x in ((whi, 0), (wlo, 0), (whi, 1)) for k in range(KC)]
                            for n_, (part, x, k) in enumerate(terms):
                                last = mm(ps[:, B_QK + n, m * N:(m + 1) * N], part[:, w, k, m * P:(m + 1) * P],
                                          h1T[:, i0, x, k, :], start=(n_ == 0),
                                          stop=(n_ == 3 * KC - 1))
                    last.then_inc(s["qk_mm"], 1)
                if live(0):
                    after(pe, "sdlo_done", a)
                    nc.tensor.transpose(sdT_bank, sdn[:, i0].rearrange("p r m -> p (r m)"), identb[:]).then_inc(s["sdT_mm"], 1)
                if live(1):
                    after(pe, "p0a_done", b_)
                    after(pe, "tg_done", a)
                    after(pe, "hp_done", a)
                    for h in range(A):
                        if h == 2 * AB:
                            after(pe, "p0_done", b_)
                        last = nc.tensor.transpose(bank(B_P0T + h // AB, k=AB)[:, h % AB, :], p0[:, i1, h, :], ident[:])
                        if h == 2 * AB - 1:
                            last.then_inc(s["p0Ta_mm"], 1)
                    last.then_inc(s["p0T_mm"], 1)
                if live(2):
                    after(pe, "res_done", t - 3)
                    after(pe, "qk_done", c)
                    mk = maskb[:, (j - 2) % 4, :].unsqueeze(1).to_broadcast([P, KC, N])
                    for n in range(HP):
                        mm(bank(B_SC + n), identb[:], mk, start=True, stop=False)
                    for h in range(HEADS):
                        q = slice(DH * (h % 2), DH * (h % 2) + DH)
                        last = mm(bank(B_SC + h % 2)[:, h // 2, :], qkT[q, i0, 0, h // 2, :], qkT[q, i0, 1, h // 2, :],
                                  start=False, stop=(h >= HEADS - HP))
                    last.then_inc(s["sc_mm"], 1)
                if live(1):
                    after(pe, "p0Ta_done", b_)
                    for h in range(A):
                        if h == 2 * AB:
                            after(pe, "p0T_done", b_)
                        last = mm(ps[:, B_PV0, h * (E + 1):(h + 1) * (E + 1)], p0T[:, i1, h, :], hp[:, i1, h, :],
                                  start=True, stop=True)
                    last.then_inc(s["pv0_mm"], 1)
                if live(-1):
                    after(pe, "h0_done", t + 1)
                    after(pe, "tg_done", t)
                    after(pe, "p0T_done", b_)
                    transposes(bank(B_H0T), h0[:, (j + 1) % 4, :]).then_inc(s["h0T_mm"], 1)
                if live(0):
                    after(pe, "sd_done", a)
                    after(pe, "mask_done", a)
                    after(pe, "v_done", t - 2)
                    mk = maskb[:, j, :].unsqueeze(1).to_broadcast([P, AB, N])
                    for n, z in enumerate(Z_BANKS):
                        zb = bank(z, k=AB)
                        mm(zb, sdp[:, i0, :], one_s[:, n * AB:(n + 1) * AB, :], start=True, stop=False)
                        mm(zb, identb[:], mk, start=False, stop=False)
                        for h in range(AB):
                            last = mm(zb[:, h, :], sel_d[:, n * AB + h, :], sdp[:, i0, :], start=False, stop=(h == AB - 1))
                    last.then_inc(s["z_mm"], 1)
            steps(pe, body)


def kernel(x, adj, L0_gnn_W, L0_gnn_b, L0_gnn_w_src, L0_gnn_w_dst, L0_gnn_H_w, L0_gnn_H_b, L1_gnn_Wq, L1_gnn_bq,
           L1_gnn_Wk, L1_gnn_bk, L1_gnn_Wv, L1_gnn_bv, L1_gnn_Wf, L1_gnn_bf):
    import numpy as np
    import concourse.bacc as bacc
    from concourse import mybir as mb
    from concourse.bass_utils import run_bass_kernel_spmd

    def rows(w):
        return np.ascontiguousarray(np.asarray(w).reshape(3, 128, -1).transpose(1, 0, 2))

    def cols(v):
        return np.ascontiguousarray(np.asarray(v).reshape(3, 128).T)

    W = np.asarray(L0_gnn_W)
    arrays = {
        "x": np.asarray(x), "adj": np.asarray(adj),
        "W": rows(W.transpose(1, 0, 2).reshape(384, 384)),
        "b": np.asarray(L0_gnn_b), "w_src": np.asarray(L0_gnn_w_src).reshape(-1),
        "w_dst": np.asarray(L0_gnn_w_dst).reshape(-1),
        "HwT": rows(np.asarray(L0_gnn_H_w).T), "H_b": np.asarray(L0_gnn_H_b),
        "Wq": rows(L1_gnn_Wq), "bq": cols(L1_gnn_bq), "Wk": rows(L1_gnn_Wk), "bk": cols(L1_gnn_bk),
        "Wv": rows(L1_gnn_Wv), "bv": np.asarray(L1_gnn_bv), "Wf": rows(L1_gnn_Wf), "bf": np.asarray(L1_gnn_bf),
    }
    nc = bacc.Bacc("TRN2", target_bir_lowering=False, num_devices=1)
    drams = {}
    for name, v in arrays.items():
        drams[name] = nc.dram_tensor(f"in_{name}", v.shape, mb.dt.from_np(v.dtype), kind="ExternalInput").ap()
    shape = arrays["x"].shape
    out = nc.dram_tensor("out_x", shape, mb.dt.float32, kind="ExternalOutput").ap()
    program(nc, out=out, **drams)
    r = run_bass_kernel_spmd(nc, [{f"in_{k}": v for k, v in arrays.items()}], core_ids=[0])
    return r.results[0]["out_x"]
```

```python
from contextlib import ExitStack

import concourse.bass as bass
from concourse import mybir

ALU = mybir.AluOpType
ACT = mybir.ActivationFunctionType
AX_X = mybir.AxisListType.X
F32 = mybir.dt.float32
BF16 = mybir.dt.bfloat16
F16 = mybir.dt.float16
I32 = mybir.dt.int32
RMAX = bass.bass_isa.ReduceOp.max
U8 = mybir.dt.uint8

P = 128
UNROLL = 4
EPS = 1e-5
MASKED0 = -999.0
NEG = -9e15
SLOPE = 0.2
PS = 1024.0
HS = 1024.0
W_TOP = 2.0 ** 13
V_TOP = 2.0 ** 5
W_H, W_G, W_Q, W_K, W_V, W_F, V0, V1, M_GB = range(9)


def program(nc, x, adj, W, b, w_src, w_dst, HwT, H_b, Wq, bq, Wk, bk, Wv, bv, Wf, bf, out):
    NB, N, D = x.shape
    E = b.shape[0]
    A = D // E
    HEADS = 6
    DH = D // HEADS
    KC = D // P
    HP = P // DH
    AB = 512 // N
    assert N == P and KC == 3 and A == 12 and E == 32 and HP == 2 and NB % UNROLL == 0
    SCALE = float(DH) ** -0.5

    with ExitStack() as ctx:
        def sb(name, shape, dt=F32):
            return ctx.enter_context(nc.sbuf_tensor(name, shape, dt))

        def sem(name):
            return ctx.enter_context(nc.semaphore(name))

        ident = sb("ident", [P, P])
        identb = sb("identb", [P, P], BF16)
        whi = sb("whi", [P, 6, KC, D], F16)
        wlo = sb("wlo", [P, 6, KC, D], F16)
        wmax = sb("wmax", [P, 9])
        wall = sb("wall", [P, 9])
        scl = sb("scl", [P, 8])
        inv = sb("inv", [P, 8])
        fac = sb("fac", [P, 8])
        qkb = sb("qkb", [P, 2, KC])
        bvr = sb("bvr", [P, D])
        bfr = sb("bfr", [P, D])
        b0r = sb("b0r", [P, E])
        w_ds = sb("w_ds", [P, 2, D])
        sel_d = sb("sel_d", [96, A, P], BF16)
        one_s = sb("one_s", [96, A, P], BF16)
        sel_b = sb("sel_b", [96, P], BF16)
        hb = sb("hb", [96, D])
        hbp = sb("hbp", [96, D], BF16)
        hbr = sb("hbr", [96, D])
        hbm = sb("hbm", [96, D], BF16)
        mhalf = sb("mhalf", [P, 1])

        xin = sb("xin", [P, 4, D])
        adj8 = sb("adj8", [P, 4, N], U8)
        maskb = sb("maskb", [P, 4, N], BF16)
        h0 = sb("h0", [P, 4, D])
        xh = sb("xh", [P, 2, D])
        tg = sb("tg", [P, 2, D])
        sg = sb("sg", [P, 2, D])
        hq = sb("hq", [P, 2, D])
        c0 = sb("c0", [P, 2, D])
        h0T = sb("h0T", [P, 2, 2, KC, N], F16)
        th = sb("th", [P, 2, D])
        ths = sb("ths", [P, 2, D])
        hs = sb("hs", [P, 2, A, E])
        hp32 = sb("hp32", [P, 2, A, E])
        hp = sb("hp", [P, 2, 2, A, E + 1], F16)
        sd32 = sb("sd32", [P, 2 * A])
        sdn = sb("sdn", [P, 2, 3, 32], BF16)
        sdp = sb("sdp", [96, 2, N], BF16)
        u2 = sb("u2", [P, 2, A, N])
        lk = sb("lk", [P, 2, A, N])
        p0 = sb("p0", [P, 2, A, N])
        p0T = sb("p0T", [P, 2, 2, A, N], F16)
        mx0 = sb("mx0", [P, 2, A])
        rd0 = sb("rd0", [P, 2, A])
        feat = sb("feat", [P, 2, D])
        fpos = sb("fpos", [P, 2, D])
        fexp = sb("fexp", [P, 2, D])
        eg = sb("eg", [P, 2, D])
        x1 = sb("x1", [P, 2, D])
        x1b = sb("x1b", [P, 2, D])
        h1 = sb("h1", [P, 2, D])
        h1T = sb("h1T", [P, 2, 2, KC, N], F16)
        qkT = sb("qkT", [P, 2, 2, KC, N])
        vs = sb("vs", [P, 2, D])
        vp32 = sb("vp32", [P, 2, D])
        vp = sb("vp", [P, 2, 2, HEADS, DH + 1], F16)
        p1 = sb("p1", [P, 2, HP, KC, N])
        p1T = sb("p1T", [P, 2, 2, HP, KC, N], F16)
        mx1 = sb("mx1", [P, 2, HP, KC])
        mxn = sb("mxn", [P, 2, HP, KC])
        rd1 = sb("rd1", [P, 2, HEADS])
        cx = sb("cx", [P, 2, D])
        cxT = sb("cxT", [P, 2, 2, KC, N], F16)
        outs = sb("outs", [P, 2, D])
        res = sb("res", [P, 2, D])
        bst = [sb(f"bst{i}", [P, 2, 6]) for i in range(2)]
        mv = [sb(f"mv{i}", [P, 2, 2]) for i in range(2)]
        ve = [sb(f"ve{i}", [P, 2, 1]) for i in range(2)]
        rstd = [sb(f"rstd{i}", [P, 2, 1]) for i in range(2)]
        nmr = [sb(f"nmr{i}", [P, 2, 1]) for i in range(2)]

        ps = ctx.enter_context(nc.psum_tensor("ps", [P, 8, 512], F32))

        def bank(i, n=N, k=KC):
            return ps[:, i, 0:k * n].rearrange("p (c n) -> p c n", n=n)

        B_H0T, B_GATE, B_H, B_SD, B_CTXT, B_OUT, B_PV1, B_PV0, B_H1T, B_V = 5, 3, 7, 2, 1, 4, 0, 5, 0, 6
        B_P1T, B_QK, B_P0T, B_SC = 0, 0, (5, 6, 4), 0
        Z_BANKS = (2, 3, 7)

        def w32(m):
            return (u2, p0, lk)[m // 2][:, m % 2, 0:KC * D // N, :].rearrange("p a n -> p (a n)").rearrange(
                "p (c n) -> p c n", n=D)

        p1T_banks = ps[:, B_P1T:B_P1T + 2, 0:KC * N].rearrange("p b (c n) -> p b c n", n=N)
        p0T_banks = {"a": ps[:, B_P0T[0]:B_P0T[0] + 2, :].rearrange("p b (c n) -> p (b c) n", n=N),
                     "": bank(B_P0T[2], k=AB)}
        heads_of = {"a": slice(0, 2 * AB), "": slice(2 * AB, A)}
        sdT_bank = ps[0:96, B_SD, 0:N // 2].bitcast(BF16)

        w_loaded = [sem(f"w_loaded{i}") for i in range(14)]
        setup_pool = sem("setup_pool")
        setup_dve = sem("setup_dve")
        maxima_done = sem("maxima_done")
        maxima_spread = sem("maxima_spread")
        scales_done = sem("scales_done")
        weights_done = sem("weights_done")
        x_loaded = [sem(f"x_loaded{i}") for i in range(4)]
        adj_loaded = [sem(f"adj_loaded{i}") for i in range(4)]
        stored = [sem(f"stored{i}") for i in range(2)]
        names = """
            bn0_done aggr0_done ve0_done rstd0_done nmr0_done h0_done xh_done mask_done
            h0T_mm h0Th_done h0T_done H_mm th_done hs_done hph_done hp_done hpl_done
            gate_mm tg_done sg_done hq_done hg_done c0_done
            ths_done sd32_done sdhi_done sdr1_done sdmid_done sdlo_done sdT_mm sd_done
            z_mm u2a_done u2_done lka_done lk_done mx0a_done mx0_done p0a_done p0_done
            p0Ta_mm p0T_mm p0Tah_done p0Th_done p0Ta_done p0T_done
            pv0_mm rd0_done feat_done fpos_done fexp_done elu_done eg_done x1_done
            bn1_done aggr1_done ve1_done rstd1_done nmr1_done h1_done x1b_done h1T_mm h1Th_done h1T_done
            qk_mm qk_done v_mm vs_done vh_done v_done vl_done sc_mm mx1_done mxn_done p1_done
            p1T_mm p1Th_done p1T_done pv1_mm rd1_done cx_done cxT_mm cxTh_done cxT_done
            out_mm outs_done res_done""".split()
        s = {n: sem(n) for n in names}

        def after(eng, name, g):
            if not isinstance(g, int) or 0 <= g < NB:
                eng.wait_ge(s[name], g + 1)

        def steps(eng, body):
            def fixed(t):
                body(t, t % UNROLL, t // UNROLL, lambda k: 0 <= t - k < NB)
            for t in range(-1, 2 * UNROLL):
                fixed(t)
            with eng.Fori(2, NB // UNROLL - 1) as turn:
                for j in range(UNROLL):
                    body(turn * UNROLL + j, j, turn, lambda k: True)
            for t in range(NB - UNROLL, NB + 3):
                fixed(t)

        block = ctx.enter_context(nc.Block())

        @block.sync
        def _(sp):
            def load(g, slot):
                sp.dma_start(xin[:, slot, :], x[g]).then_inc(x_loaded[slot], 16)
                sp.dma_start(adj8[:, slot, :], adj[g]).then_inc(adj_loaded[slot], 16)
            def on_rows(v, rows):
                return v.rearrange("(o n) -> o n", o=1).to_broadcast([rows, v.shape[0]])
            load(0, 0)
            for n, (dst, src) in enumerate([
                    (w32(W_H), W), (w32(W_G), HwT), (w32(W_Q), Wq), (w32(W_K), Wk), (w32(W_V), Wv), (w32(W_F), Wf),
                    (hb[:], on_rows(H_b, 96)), (b0r[:], on_rows(b, P)), (bvr[:], on_rows(bv, P)),
                    (w_ds[:, 0, :], on_rows(w_dst, P)), (w_ds[:, 1, :], on_rows(w_src, P)),
                    (qkb[:, 0, :], bq), (qkb[:, 1, :], bk), (bfr[:], on_rows(bf, P))]):
                sp.dma_start(dst, src).then_inc(w_loaded[n], 16)
            load(1, 1)

            def body(t, j, turn, live):
                if live(-2):
                    after(sp, "xh_done", t - 2)
                    after(sp, "mask_done", t - 2)
                    load(t + 2, (j + 2) % 4)
                if live(3):
                    after(sp, "res_done", t - 3)
                    sp.dma_start(out[t - 3], res[:, (j - 3) % 2, :]).then_inc(stored[(j - 3) % 2], 16)
            steps(sp, lambda t, j, turn, live: None if isinstance(t, int) and t < 0 else body(t, j, turn, live))
            for i in range(2):
                sp.wait_ge(stored[i], 16 * (NB // 2))

        @block.gpsimd
        def _(pool):
            for n, m in enumerate((ident, identb, sel_d, one_s, sel_b)):
                nc.gpsimd.memset(m[:], 0.0).then_inc(setup_pool, 1)
            nc.gpsimd.memset(mhalf[:], -0.5).then_inc(setup_pool, 1)
            for m in (hp, vp):
                nc.gpsimd.memset(m[:, :, 0], 1.0).then_inc(setup_pool, 1)
                nc.gpsimd.memset(m[:, :, 1], 0.0).then_inc(setup_pool, 1)
            pool.wait_ge(setup_pool, 10)
            count = 10
            for m in (ident, identb):
                nc.gpsimd.affine_select(out=m[:], in_=m[:], compare_op=ALU.not_equal, fill=1.0, base=0,
                                        pattern=[[-1, P]], channel_multiplier=1).then_inc(setup_pool, 1)
                count += 1
            for r in range(3):
                for m, first in ((sel_d, 0), (one_s, A)):
                    nc.gpsimd.affine_select(out=m[:], in_=m[:], compare_op=ALU.not_equal, fill=1.0,
                                            base=-(32 * r + first), pattern=[[-1, A], [0, P]],
                                            channel_multiplier=1).then_inc(setup_pool, 1)
                    count += 1
                    pool.wait_ge(setup_pool, count)
                nc.gpsimd.affine_select(out=sel_b[:], in_=sel_b[:], compare_op=ALU.not_equal, fill=1.0,
                                        base=-32 * r, pattern=[[0, P]], channel_multiplier=1).then_inc(setup_pool, 1)
                count += 1
                pool.wait_ge(setup_pool, count)
            nc.gpsimd.memset(sdn[:], 0.0).then_inc(setup_pool, 1)
            pool.wait_ge(maxima_done, 1)
            nc.gpsimd.partition_all_reduce(wall[:], wmax[:], P, RMAX).then_inc(maxima_spread, 1)
            for n in (9, 10, 13):
                pool.wait_ge(w_loaded[n], 16)
            pool.wait_ge(scales_done, 1)

            def body(t, j, turn, live):
                if live(0):
                    after(pool, "th_done", t)
                    after(pool, "sd32_done", t - 1)
                    nc.gpsimd.tensor_tensor(ths[:], th[:, j % 2, :].unsqueeze(1).to_broadcast([P, 2, D]), w_ds[:],
                                            ALU.mult).then_inc(s["ths_done"], 1)
                if live(3):
                    after(pool, "vh_done", t - 3)
                    after(pool, "v_done", t - 3)
                    nc.gpsimd.tensor_tensor(vp[:, (j - 3) % 2, 1, :, 0:DH],
                                            vp32[:, (j - 3) % 2, :].rearrange("p (h e) -> p h e", e=DH),
                                            vp[:, (j - 3) % 2, 0, :, 0:DH],
                                            ALU.subtract).then_inc(s["vl_done"], 1)
                if live(-1):
                    g, i, k = t + 1, (j + 1) % 2, (j + 1) % 4
                    pool.wait_ge(adj_loaded[k], 16 * (turn + (1 if j == 3 else 0)) + 16)
                    after(pool, "sc_mm", g - 4)
                    after(pool, "ve0_done", g)
                    nc.gpsimd.tensor_tensor(rstd[0][:, i, :], ve[0][:, i, :], mhalf[:], ALU.pow).then_inc(s["rstd0_done"], 1)
                    nc.gpsimd.tensor_scalar(maskb[:, k, :], adj8[:, k, :], -1.0, -NEG, ALU.add,
                                            ALU.mult).then_inc(s["mask_done"], 1)
                if live(0):
                    after(pool, "pv0_mm", t - 2)
                    after(pool, "hs_done", t)
                    nc.gpsimd.tensor_tensor(hp[:, j % 2, 0, :, 0:E], hs[:, j % 2],
                                            b0r[:].unsqueeze(1).to_broadcast([P, A, E]),
                                            ALU.add).then_inc(s["hph_done"], 1)
                    nc.gpsimd.tensor_tensor(hp32[:, j % 2], hs[:, j % 2], b0r[:].unsqueeze(1).to_broadcast([P, A, E]),
                                            ALU.add).then_inc(s["hp_done"], 1)
                if live(2):
                    g, i = t - 2, (j - 2) % 2
                    after(pool, "ve1_done", g)
                    nc.gpsimd.tensor_tensor(rstd[1][:, i, :], ve[1][:, i, :], mhalf[:], ALU.pow).then_inc(s["rstd1_done"], 1)
                if live(2):
                    g, i = t - 2, (j - 2) % 2
                    after(pool, "x1_done", g)
                    after(pool, "res_done", g - 2)
                    nc.gpsimd.tensor_tensor(x1b[:, i, :], x1[:, i, :], bfr[:], ALU.add).then_inc(s["x1b_done"], 1)
                if live(1):
                    after(pool, "tg_done", t - 1)
                if live(0):
                    after(pool, "c0_done", t - 2)
                    after(pool, "h0_done", t)
                    nc.gpsimd.tensor_tensor(xh[:, j % 2, :], xin[:, j, :], h0[:, j, :], ALU.add).then_inc(s["xh_done"], 1)
                if live(1):
                    g, i, k = t - 1, (j - 1) % 2, (j - 1) % 4
                    nc.gpsimd.tensor_scalar(sg[:, i, :], tg[:, i, :], 1.0, 0.5, ALU.add, ALU.mult).then_inc(s["sg_done"], 1)
                    nc.gpsimd.tensor_scalar(hq[:, i, :], h0[:, k, :], 1.0, 1.0, ALU.add, ALU.mult).then_inc(s["hq_done"], 1)
                    after(pool, "sg_done", g)
                    after(pool, "hq_done", g)
                    nc.gpsimd.tensor_tensor(hq[:, i, :], hq[:, i, :], sg[:, i, :], ALU.mult).then_inc(s["hg_done"], 1)
                    after(pool, "hg_done", g)
                    nc.gpsimd.tensor_tensor(c0[:, i, :], xh[:, i, :], hq[:, i, :], ALU.subtract).then_inc(s["c0_done"], 1)
                if live(3):
                    after(pool, "x1b_done", t - 3)
                    after(pool, "outs_done", t - 3)
                    if not isinstance(t, int) or t - 3 >= 2:
                        pool.wait_ge(stored[(j - 3) % 2], 32 * turn + 16 * ((j - 3) // 2))
                    nc.gpsimd.tensor_tensor(res[:, (j - 3) % 2, :], outs[:, (j - 3) % 2, :], x1b[:, (j - 3) % 2, :],
                                            ALU.add).then_inc(s["res_done"], 1)
                if live(0):
                    after(pool, "hph_done", t)
                    after(pool, "hp_done", t)
                    nc.gpsimd.tensor_tensor(hp[:, j % 2, 1, :, 0:E], hp32[:, j % 2], hp[:, j % 2, 0, :, 0:E],
                                            ALU.subtract).then_inc(s["hpl_done"], 1)
                if live(2):
                    after(pool, "pv1_mm", t - 4)
                    after(pool, "vs_done", t - 2)
                    nc.gpsimd.tensor_tensor(vp[:, j % 2, 0, :, 0:DH], vs[:, j % 2, :].rearrange("p (h e) -> p h e", e=DH),
                                            bvr[:].rearrange("p (h e) -> p h e", e=DH), ALU.add).then_inc(s["vh_done"], 1)
                    nc.gpsimd.tensor_tensor(vp32[:, j % 2, :], vs[:, j % 2, :], bvr[:], ALU.add).then_inc(s["v_done"], 1)
            steps(pool, body)

        @block.scalar
        def _(act):
            act.wait_ge(scales_done, 1)
            act.wait_ge(weights_done, 1)

            def body(t, j, turn, live):
                a, b_, c, d = t, t - 1, t - 2, t - 3
                i0, i1 = j % 2, (j + 1) % 2
                if live(2):
                    after(act, "feat_done", c)
                    nc.scalar.activation(fexp[:, i0, :], feat[:, i0, :], ACT.Exp).then_inc(s["fexp_done"], 1)
                if live(1):
                    after(act, "p0T_mm", b_ - 2)
                    after(act, "mx0_done", b_)
                    for h in range(2 * AB, A):
                        last = nc.scalar.activation(p0[:, i1, h, :], lk[:, i1, h, :], ACT.Exp, bias=mx0[:, i1, h:h + 1])
                    last.then_inc(s["p0_done"], 1)
                if live(3):
                    after(act, "p1T_mm", d)
                    nc.scalar.mul(p1T[:, i1, 0], p1T_banks, PS).then_inc(s["p1Th_done"], 1)
                if live(0):
                    after(act, "gate_mm", a)
                    after(act, "sg_done", a - 2)
                    nc.scalar.activation(tg[:, i0, :], ps[:, B_GATE, 0:D], ACT.Tanh,
                                         scale=fac[:, W_G:W_G + 1]).then_inc(s["tg_done"], 1)
                if live(1):
                    for part, heads in heads_of.items():
                        after(act, f"p0T{part}_mm", b_)
                        nc.scalar.mul(p0T[:, i1, 0, heads, :], p0T_banks[part], PS).then_inc(s[f"p0T{part}h_done"], 1)
                if live(0):
                    after(act, "sdT_mm", a)
                    after(act, "z_mm", a - 2)
                    nc.scalar.copy(sdp[:, i0, :], sdT_bank).then_inc(s["sd_done"], 1)
                if live(-1):
                    after(act, "nmr0_done", t + 1)
                    after(act, "hq_done", t - 3)
                    after(act, "xh_done", t - 3)
                    nc.scalar.activation(h0[:, (j + 1) % 4, :], xin[:, (j + 1) % 4, :], ACT.Relu,
                                         bias=nmr[0][:, i1, :], scale=rstd[0][:, i1, :]).then_inc(s["h0_done"], 1)
                if live(2):
                    after(act, "nmr1_done", c)
                    after(act, "h1T_mm", c - 2)
                    nc.scalar.activation(h1[:, i0, :], x1[:, i0, :], ACT.Relu, bias=nmr[1][:, i0, :],
                                         scale=rstd[1][:, i0, :]).then_inc(s["h1_done"], 1)
                if live(3):
                    after(act, "cxT_mm", d)
                    nc.scalar.copy(cxT[:, i1, 0], bank(B_CTXT)).then_inc(s["cxTh_done"], 1)
                if live(2):
                    after(act, "h1T_mm", c)
                    nc.scalar.mul(h1T[:, i0, 0], bank(B_H1T), HS).then_inc(s["h1Th_done"], 1)
                if live(0):
                    after(act, "z_mm", a)
                    after(act, "lk_done", a - 2)
                    after(act, "lka_done", a - 2)
                    nc.scalar.mul(u2[:, i0, 2 * AB:A, :], bank(Z_BANKS[2], k=AB), SLOPE).then_inc(s["u2_done"], 1)
                    nc.scalar.mul(u2[:, i0, 0:2 * AB, :],
                                  ps[:, Z_BANKS[0]:Z_BANKS[0] + 2, :].rearrange("p b (c n) -> p (b c) n", n=N),
                                  SLOPE).then_inc(s["u2a_done"], 1)
                if live(3):
                    after(act, "out_mm", d)
                    nc.scalar.activation(outs[:, i1, :], ps[:, B_OUT, 0:D], ACT.Identity,
                                         scale=fac[:, W_F:W_F + 1]).then_inc(s["outs_done"], 1)
                if live(-1):
                    after(act, "h0T_mm", t + 1)
                    nc.scalar.mul(h0T[:, i1, 0], bank(B_H0T), HS).then_inc(s["h0Th_done"], 1)
                if live(2):
                    after(act, "v_mm", c)
                    nc.scalar.activation(vs[:, i0, :], ps[:, B_V, 0:D], ACT.Identity,
                                         scale=fac[:, W_V:W_V + 1]).then_inc(s["vs_done"], 1)
                if live(0):
                    after(act, "p0T_mm", a - 2)
                    after(act, "mx0a_done", a)
                    for h in range(0, 2 * AB):
                        last = nc.scalar.activation(p0[:, i0, h, :], lk[:, i0, h, :], ACT.Exp, bias=mx0[:, i0, h:h + 1])
                    last.then_inc(s["p0a_done"], 1)
                if live(-1):
                    after(act, "H_mm", t + 1)
                    after(act, "ths_done", t - 1)
                    nc.scalar.activation(th[:, i1, :], ps[:, B_H, 0:D], ACT.Tanh,
                                         scale=inv[:, W_H:W_H + 1]).then_inc(s["th_done"], 1)
                if live(2):
                    after(act, "mxn_done", c)
                    after(act, "p1T_mm", c - 2)
                    for h in range(HEADS):
                        n, m = h % 2, h // 2
                        last = nc.scalar.activation(p1[:, i0, n, m, :], bank(B_SC + n)[:, m, :], ACT.Exp,
                                                    bias=mxn[:, i0, n, m:m + 1], scale=SCALE)
                    last.then_inc(s["p1_done"], 1)
                if live(-1):
                    after(act, "H_mm", t + 1)
                    after(act, "hp_done", t - 1)
                    nc.scalar.activation(hs[:, i1], ps[:, B_H, 0:D].rearrange("p (a e) -> p a e", e=E), ACT.Identity,
                                         scale=fac[:, W_H:W_H + 1]).then_inc(s["hs_done"], 1)
            steps(act, body)

        @block.vector
        def _(dve):
            count = 0

            def chain(instruction):
                nonlocal count
                count += 1
                instruction.then_inc(setup_dve, 1)
                dve.wait_ge(setup_dve, count)

            ts, tt, stt = nc.vector.tensor_scalar, nc.vector.tensor_tensor, nc.vector.scalar_tensor_tensor
            chain(nc.vector.memset(wmax[:], 0.0))
            for n, (col, src) in enumerate([(m, w32(m).rearrange("p c n -> p (c n)")) for m in range(6)]
                                           + [(M_GB, hb[:]), (V0, b0r[:]), (V1, bvr[:])]):
                dve.wait_ge(w_loaded[n], 16)
                last = nc.vector.tensor_reduce(wmax[0:src.shape[0], col:col + 1], src, AX_X, ALU.max,
                                               apply_absolute_value=True)
            last.then_inc(maxima_done, 1)
            dve.wait_ge(maxima_spread, 1)
            for dst, src in ((V0, W_H), (V1, W_V), (W_G, M_GB), (W_Q, W_K)):
                chain(tt(wall[:, dst:dst + 1], wall[:, dst:dst + 1], wall[:, src:src + 1], ALU.max))
            chain(nc.vector.tensor_copy(wall[:, W_K:W_K + 1], wall[:, W_Q:W_Q + 1]))
            chain(ts(wall[:], wall[:], 1e-30, None, ALU.max))
            chain(ts(wall[:].bitcast(I32), wall[:].bitcast(I32), 0x7F800000, None, ALU.bitwise_and))
            chain(nc.vector.reciprocal(scl[:], wall[:, 0:8]))
            chain(ts(scl[:, 0:6], scl[:, 0:6], W_TOP, None, ALU.mult))
            chain(ts(scl[:, 6:8], scl[:, 6:8], V_TOP, None, ALU.mult))
            chain(ts(inv[:, 0:6], wall[:, 0:6], 1.0 / (W_TOP * HS), None, ALU.mult))
            chain(ts(inv[:, 6:8], wall[:, 6:8], 1.0 / V_TOP, None, ALU.mult))
            for dst, f, other in ((W_H, inv, scl[:, V0:V0 + 1]), (W_V, inv, scl[:, V1:V1 + 1])):
                chain(tt(fac[:, dst:dst + 1], f[:, dst:dst + 1], other, ALU.mult))
            chain(stt(fac[:, W_F:W_F + 1], inv[:, W_F:W_F + 1], HS, inv[:, V1:V1 + 1], ALU.mult, ALU.mult))
            chain(ts(fac[:, W_G:W_G + 1], inv[:, W_G:W_G + 1], 0.5, None, ALU.mult))
            chain(ts(b0r[:], b0r[:], scl[:, V0:V0 + 1], None, ALU.mult))
            chain(ts(bvr[:], bvr[:], scl[:, V1:V1 + 1], None, ALU.mult))
            for n in (11, 12):
                dve.wait_ge(w_loaded[n], 16)
            dve.wait_ge(setup_pool, 22)
            chain(ts(hb[:], hb[:], scl[0:96, W_G:W_G + 1], HS, ALU.mult, ALU.mult))
            nc.vector.tensor_copy(hbp[:], hb[:]).then_inc(scales_done, 1)
            dve.wait_ge(scales_done, 1)
            chain(tt(hbr[:], hb[:], hbp[:], ALU.subtract))
            chain(nc.vector.tensor_copy(hbm[64:96], hbr[64:96]))
            chain(nc.vector.tensor_copy(hbp[32:64], hbr[32:64]))
            chain(tt(hbp[64:96], hbr[64:96], hbm[64:96], ALU.subtract))
            for m in range(6):
                chain(ts(whi[:, m], w32(m), scl[:, m:m + 1], None, ALU.mult))
                last = stt(wlo[:, m], w32(m), scl[:, m:m + 1], whi[:, m], ALU.mult, ALU.subtract)
            last.then_inc(weights_done, 1)

            def norm(k, src, g, i, between):
                nc.vector.bn_stats(bst[k][:, i, :], src).then_inc(s[f"bn{k}_done"], 1)
                after(dve, f"bn{k}_done", g)
                between()
                nc.vector.bn_aggr(mv[k][:, i, :], bst[k][:, i, :]).then_inc(s[f"aggr{k}_done"], 1)
                after(dve, f"aggr{k}_done", g)
                nc.vector.tensor_scalar(ve[k][:, i, :], mv[k][:, i, 1:2], EPS, None, ALU.add).then_inc(s[f"ve{k}_done"], 1)

            def norm_bias(k, g, i):
                after(dve, f"rstd{k}_done", g)
                nc.vector.scalar_tensor_tensor(nmr[k][:, i, :], mv[k][:, i, 0:1], -1.0, rstd[k][:, i, :],
                                               ALU.mult, ALU.mult).then_inc(s[f"nmr{k}_done"], 1)

            def low_part(name, low, source, scale, high, g):
                after(dve, f"{name}h_done", g)
                nc.vector.scalar_tensor_tensor(low, source, scale, high, ALU.mult,
                                               ALU.subtract).then_inc(s[f"{name}_done"], 1)

            pv0 = ps[:, B_PV0, 0:A * (E + 1)].rearrange("p (a e) -> p a e", e=E + 1)
            pv1 = ps[:, B_PV1, 0:HEADS * (DH + 1)].rearrange("p (h e) -> p h e", e=DH + 1)

            def body(t, j, turn, live):
                a, b_, c, d = t, t - 1, t - 2, t - 3
                i0, i1 = j % 2, (j + 1) % 2
                def row_sums():
                    if live(2):
                        after(dve, "pv0_mm", c)
                        nc.vector.reciprocal(rd0[:, i0, :], pv0[:, :, E:E + 1]).then_inc(s["rd0_done"], 1)
                if live(-1):
                    k = (j + 1) % 4
                    dve.wait_ge(x_loaded[k], 16 * (turn + (1 if j == 3 else 0)) + 16)
                    norm(0, xin[:, k, :], t + 1, i1, row_sums)
                else:
                    row_sums()
                if live(2):
                    after(dve, "rd0_done", c)
                    nc.vector.scalar_tensor_tensor(feat[:, i0, :].rearrange("p (a e) -> p a e", e=E), pv0[:, :, 0:E],
                                                   inv[:, V0:V0 + 1], rd0[:, i0, :].unsqueeze(2).to_broadcast([P, A, E]),
                                                   ALU.mult, ALU.mult).then_inc(s["feat_done"], 1)
                    after(dve, "feat_done", c)
                    nc.vector.tensor_scalar(fpos[:, i0, :], feat[:, i0, :], 0.0, None, ALU.max).then_inc(s["fpos_done"], 1)
                if live(0):
                    after(dve, "ths_done", a)
                    nc.vector.tensor_reduce(sd32[:], ths[:].rearrange("p k (a e) -> p (k a) e", e=E), AX_X,
                                            ALU.add).then_inc(s["sd32_done"], 1)
                if live(2):
                    after(dve, "fpos_done", c)
                    after(dve, "fexp_done", c)
                    nc.vector.scalar_tensor_tensor(eg[:, i0, :], fexp[:, i0, :], 1.0, fpos[:, i0, :], ALU.min,
                                                   ALU.add).then_inc(s["elu_done"], 1)
                if live(0):
                    after(dve, "sd32_done", a)
                    after(dve, "sdT_mm", a - 2)
                    nc.vector.tensor_copy(sdn[:, i0, 0, 0:2 * A], sd32[:]).then_inc(s["sdhi_done"], 1)
                if live(2):
                    after(dve, "elu_done", c)
                    after(dve, "c0_done", c)
                    nc.vector.tensor_tensor(eg[:, i0, :], eg[:, i0, :], sg[:, i0, :], ALU.mult).then_inc(s["eg_done"], 1)
                if live(0):
                    after(dve, "sdhi_done", a)
                    nc.vector.tensor_tensor(sd32[:], sd32[:], sdn[:, i0, 0, 0:2 * A],
                                            ALU.subtract).then_inc(s["sdr1_done"], 1)
                if live(2):
                    after(dve, "eg_done", c)
                    after(dve, "x1b_done", c - 2)
                    after(dve, "h1_done", c - 2)
                    nc.vector.tensor_tensor(x1[:, i0, :], eg[:, i0, :], c0[:, i0, :], ALU.add).then_inc(s["x1_done"], 1)
                if live(0):
                    after(dve, "sdr1_done", a)
                    nc.vector.tensor_copy(sdn[:, i0, 1, 0:2 * A], sd32[:]).then_inc(s["sdmid_done"], 1)
                    after(dve, "sdmid_done", a)
                    nc.vector.tensor_tensor(sdn[:, i0, 2, 0:2 * A], sd32[:], sdn[:, i0, 1, 0:2 * A],
                                            ALU.subtract).then_inc(s["sdlo_done"], 1)
                if live(-1):
                    norm_bias(0, t + 1, i1)
                if live(3):
                    low_part("p1T", p1T[:, i1, 1], p1T_banks, PS, p1T[:, i1, 0], d)
                if live(2):
                    after(dve, "x1_done", c)
                    nc.vector.bn_stats(bst[1][:, i0, :], x1[:, i0, :]).then_inc(s["bn1_done"], 1)
                    after(dve, "bn1_done", c)
                if live(3):
                    after(dve, "pv1_mm", d)
                    nc.vector.reciprocal(rd1[:, i1, :], pv1[:, :, DH:DH + 1]).then_inc(s["rd1_done"], 1)
                if live(2):
                    nc.vector.bn_aggr(mv[1][:, i0, :], bst[1][:, i0, :]).then_inc(s["aggr1_done"], 1)
                    after(dve, "aggr1_done", c)
                    nc.vector.tensor_scalar(ve[1][:, i0, :], mv[1][:, i0, 1:2], EPS, None, ALU.add).then_inc(s["ve1_done"], 1)
                if live(3):
                    after(dve, "rd1_done", d)
                    nc.vector.tensor_tensor(cx[:, i1, :].rearrange("p (h e) -> p h e", e=DH), pv1[:, :, 0:DH],
                                            rd1[:, i1, :].unsqueeze(2).to_broadcast([P, HEADS, DH]),
                                            ALU.mult).then_inc(s["cx_done"], 1)
                if live(2):
                    norm_bias(1, c, i0)
                if live(1):
                    low_part("p0T", p0T[:, i1, 1, heads_of[""], :], p0T_banks[""], PS,
                             p0T[:, i1, 0, heads_of[""], :], b_)
                if live(3):
                    low_part("cxT", cxT[:, i1, 1], bank(B_CTXT), 1.0, cxT[:, i1, 0], d)
                if live(1):
                    low_part("p0Ta", p0T[:, i1, 1, heads_of["a"], :], p0T_banks["a"], PS,
                             p0T[:, i1, 0, heads_of["a"], :], b_)
                if live(2):
                    low_part("h1T", h1T[:, i0, 1], bank(B_H1T), HS, h1T[:, i0, 0], c)
                if live(0):
                    after(dve, "u2_done", a)
                    after(dve, "p0_done", a - 2)
                    nc.vector.scalar_tensor_tensor(lk[:, i0, 2 * AB:A, :], bank(Z_BANKS[2], k=AB), MASKED0,
                                                   u2[:, i0, 2 * AB:A, :], ALU.max, ALU.max).then_inc(s["lk_done"], 1)
                if live(0):
                    after(dve, "u2a_done", a)
                    after(dve, "p0_done", a - 2)
                    nc.vector.scalar_tensor_tensor(
                        lk[:, i0, 0:2 * AB, :],
                        ps[:, Z_BANKS[0]:Z_BANKS[0] + 2, :].rearrange("p b (c n) -> p (b c) n", n=N), MASKED0,
                        u2[:, i0, 0:2 * AB, :], ALU.max, ALU.max).then_inc(s["lka_done"], 1)
                if live(-1):
                    low_part("h0T", h0T[:, i1, 1], bank(B_H0T), HS, h0T[:, i1, 0], t + 1)
                if live(2):
                    after(dve, "qk_mm", c)
                    nc.vector.scalar_tensor_tensor(qkT[:, i0, :, :, :],
                                                   ps[:, B_QK:B_QK + 2, 0:KC * N].rearrange("p b (c n) -> p b c n", n=N),
                                                   inv[:, W_Q:W_Q + 1], qkb[:].unsqueeze(3).to_broadcast([P, 2, KC, N]),
                                                   ALU.mult, ALU.add).then_inc(s["qk_done"], 1)
                if live(0):
                    after(dve, "lka_done", a)
                    nc.vector.tensor_reduce(mx0[:, i0, 0:2 * AB], lk[:, i0, 0:2 * AB, :], AX_X, ALU.max,
                                            negate=True).then_inc(s["mx0a_done"], 1)
                if live(0):
                    after(dve, "lk_done", a)
                    nc.vector.tensor_reduce(mx0[:, i0, 2 * AB:A], lk[:, i0, 2 * AB:A, :], AX_X, ALU.max,
                                            negate=True).then_inc(s["mx0_done"], 1)
                if live(2):
                    scores = ps[:, B_SC:B_SC + 2, 0:KC * N].rearrange("p b (c n) -> p b c n", n=N)
                    after(dve, "sc_mm", c)
                    nc.vector.tensor_reduce(mx1[:, i0, :, :], scores, AX_X, ALU.max).then_inc(s["mx1_done"], 1)
                    after(dve, "mx1_done", c)
                    nc.vector.tensor_scalar(mxn[:, i0, :, :], mx1[:, i0, :, :], -SCALE, None, ALU.mult).then_inc(s["mxn_done"], 1)
            steps(dve, body)

        @block.tensor
        def _(pe):
            mm = nc.tensor.matmul
            pe.wait_ge(setup_pool, 21)
            pe.wait_ge(weights_done, 1)

            def transposes(dst, src):
                for c in range(KC):
                    last = nc.tensor.transpose(dst[:, c, :], src[:, c * P:(c + 1) * P], ident[:])
                return last

            def values_of(dst, pT, v):
                mm(dst, pT[:, 0, :], v[:, 0, :], start=True, stop=False)
                mm(dst, pT[:, 0, :], v[:, 1, :], start=False, stop=False)
                return mm(dst, pT[:, 1, :], v[:, 0, :], start=False, stop=True)

            def project(dst, name, xT, w, g, start=True):
                after(pe, f"{name}h_done", g)
                for c in range(KC):
                    for n, part in enumerate((whi, wlo)):
                        mm(dst, xT[:, 0, c, :], part[:, w, c, :], start=(start and c == 0 and n == 0), stop=False)
                after(pe, f"{name}_done", g)
                for c in range(KC):
                    last = mm(dst, xT[:, 1, c, :], whi[:, w, c, :], start=False, stop=(c == KC - 1))
                return last

            def body(t, j, turn, live):
                a, b_, c, d = t, t - 1, t - 2, t - 3
                i0, i1 = j % 2, (j + 1) % 2
                if live(0):
                    after(pe, "lka_done", t - 1)
                    mm(ps[:, B_GATE, 0:D], sel_b[:], hbp[:], start=True, stop=False)
                    project(ps[:, B_GATE, 0:D], "h0T", h0T[:, i0], W_G, a, start=False).then_inc(s["gate_mm"], 1)
                if live(3):
                    after(pe, "p1_done", d)
                    for h in range(HEADS):
                        last = nc.tensor.transpose(bank(B_P1T + h % 2)[:, h // 2, :], p1[:, i1, h % 2, h // 2, :], ident[:])
                    last.then_inc(s["p1T_mm"], 1)
                if live(1):
                    after(pe, "p0a_done", b_)
                    after(pe, "feat_done", c)
                    after(pe, "vs_done", d)
                    for h in range(A):
                        if h == 2 * AB:
                            after(pe, "outs_done", t - 4)
                            after(pe, "p0_done", b_)
                        last = nc.tensor.transpose(bank(B_P0T[h // AB], k=AB)[:, h % AB, :], p0[:, i1, h, :], ident[:])
                        if h == 2 * AB - 1:
                            last.then_inc(s["p0Ta_mm"], 1)
                    last.then_inc(s["p0T_mm"], 1)
                if live(0):
                    after(pe, "sdlo_done", a)
                    after(pe, "lka_done", t - 1)
                    nc.tensor.transpose(sdT_bank, sdn[:, i0].rearrange("p r m -> p (r m)"), identb[:]).then_inc(s["sdT_mm"], 1)
                if live(3):
                    after(pe, "p1T_done", d)
                    after(pe, "vl_done", d)
                    for h in range(HEADS):
                        last = values_of(ps[:, B_PV1, h * (DH + 1):(h + 1) * (DH + 1)],
                                         p1T[:, i1, :, h % 2, h // 2, :], vp[:, i1, :, h, :])
                    last.then_inc(s["pv1_mm"], 1)
                if live(0):
                    after(pe, "hs_done", a)
                    after(pe, "tg_done", a)
                    after(pe, "sd_done", a)
                    after(pe, "mask_done", a)
                    after(pe, "lk_done", t - 1)
                    mk = maskb[:, j, :].unsqueeze(1).to_broadcast([P, AB, N])
                    for n, z in enumerate(Z_BANKS):
                        zb = bank(z, k=AB)
                        mm(zb, sdp[:, i0, :], one_s[:, n * AB:(n + 1) * AB, :], start=True, stop=False)
                        mm(zb, identb[:], mk, start=False, stop=False)
                        for h in range(AB):
                            last = mm(zb[:, h, :], sel_d[:, n * AB + h, :], sdp[:, i0, :], start=False, stop=(h == AB - 1))
                    last.then_inc(s["z_mm"], 1)
                if live(3):
                    after(pe, "cx_done", d)
                    transposes(bank(B_CTXT), cx[:, i1, :]).then_inc(s["cxT_mm"], 1)
                if live(2):
                    after(pe, "h1_done", c)
                    after(pe, "cx_done", d)
                    transposes(bank(B_H1T), h1[:, i0, :]).then_inc(s["h1T_mm"], 1)
                if live(3):
                    after(pe, "p0T_done", b_)
                    project(ps[:, B_OUT, 0:D], "cxT", cxT[:, i1], W_F, d).then_inc(s["out_mm"], 1)
                if live(-1):
                    after(pe, "h0_done", t + 1)
                    after(pe, "p0Ta_done", b_)
                    transposes(bank(B_H0T), h0[:, (j + 1) % 4, :]).then_inc(s["h0T_mm"], 1)
                if live(2):
                    after(pe, "h1T_done", c)
                    for n, w in enumerate((W_Q, W_K)):
                        for m in range(KC):
                            terms = [(part, x, k) for part, x in ((whi, 0), (wlo, 0), (whi, 1)) for k in range(KC)]
                            for n_, (part, x, k) in enumerate(terms):
                                last = mm(ps[:, B_QK + n, m * N:(m + 1) * N], part[:, w, k, m * P:(m + 1) * P],
                                          h1T[:, i0, x, k, :], start=(n_ == 0),
                                          stop=(n_ == 3 * KC - 1))
                    last.then_inc(s["qk_mm"], 1)
                if live(2):
                    after(pe, "p0T_done", b_)
                    project(ps[:, B_V, 0:D], "h1T", h1T[:, i0], W_V, c).then_inc(s["v_mm"], 1)
                if live(2):
                    after(pe, "qk_done", c)
                    mk = maskb[:, (j - 2) % 4, :].unsqueeze(1).to_broadcast([P, KC, N])
                    for n in range(HP):
                        mm(bank(B_SC + n), identb[:], mk, start=True, stop=False)
                    for h in range(HEADS):
                        q = slice(DH * (h % 2), DH * (h % 2) + DH)
                        last = mm(bank(B_SC + h % 2)[:, h // 2, :], qkT[q, i0, 0, h // 2, :], qkT[q, i0, 1, h // 2, :],
                                  start=False, stop=(h >= HEADS - HP))
                    last.then_inc(s["sc_mm"], 1)
                if live(-1):
                    after(pe, "lk_done", t)
                    project(ps[:, B_H, 0:D], "h0T", h0T[:, i1], W_H, t + 1).then_inc(s["H_mm"], 1)
                if live(1):
                    after(pe, "p0Ta_done", b_)
                    after(pe, "hpl_done", b_)
                    after(pe, "h0T_done", t + 1)
                    for h in range(A):
                        if h == 2 * AB:
                            after(pe, "p0T_done", b_)
                        last = values_of(ps[:, B_PV0, h * (E + 1):(h + 1) * (E + 1)],
                                         p0T[:, i1, :, h, :], hp[:, i1, :, h, :])
                    last.then_inc(s["pv0_mm"], 1)
            steps(pe, body)


def kernel(x, adj, L0_gnn_W, L0_gnn_b, L0_gnn_w_src, L0_gnn_w_dst, L0_gnn_H_w, L0_gnn_H_b, L1_gnn_Wq, L1_gnn_bq,
           L1_gnn_Wk, L1_gnn_bk, L1_gnn_Wv, L1_gnn_bv, L1_gnn_Wf, L1_gnn_bf):
    import numpy as np
    import concourse.bacc as bacc
    from concourse import mybir as mb
    from concourse.bass_utils import run_bass_kernel_spmd

    def rows(w):
        return np.ascontiguousarray(np.asarray(w).reshape(3, 128, -1).transpose(1, 0, 2))

    def cols(v):
        return np.ascontiguousarray(np.asarray(v).reshape(3, 128).T)

    W = np.asarray(L0_gnn_W)
    arrays = {
        "x": np.asarray(x), "adj": np.asarray(adj),
        "W": rows(W.transpose(1, 0, 2).reshape(384, 384)),
        "b": np.asarray(L0_gnn_b), "w_src": np.asarray(L0_gnn_w_src).reshape(-1),
        "w_dst": np.asarray(L0_gnn_w_dst).reshape(-1),
        "HwT": rows(np.asarray(L0_gnn_H_w).T), "H_b": np.asarray(L0_gnn_H_b),
        "Wq": rows(L1_gnn_Wq), "bq": cols(L1_gnn_bq), "Wk": rows(L1_gnn_Wk), "bk": cols(L1_gnn_bk),
        "Wv": rows(L1_gnn_Wv), "bv": np.asarray(L1_gnn_bv), "Wf": rows(L1_gnn_Wf), "bf": np.asarray(L1_gnn_bf),
    }
    nc = bacc.Bacc("TRN2", target_bir_lowering=False, num_devices=1)
    drams = {}
    for name, v in arrays.items():
        drams[name] = nc.dram_tensor(f"in_{name}", v.shape, mb.dt.from_np(v.dtype), kind="ExternalInput").ap()
    shape = arrays["x"].shape
    out = nc.dram_tensor("out_x", shape, mb.dt.float32, kind="ExternalOutput").ap()
    program(nc, out=out, **drams)
    r = run_bass_kernel_spmd(nc, [{f"in_{k}": v for k, v in arrays.items()}], core_ids=[0])
    return r.results[0]["out_x"]
```
